# Optimizing a Trainium2 kernel written in Bass

```python
import numpy as np
import jax
import jax.numpy as jnp

def _softmax(x, axis=-1):
    return jax.nn.softmax(x, axis=axis)

def _gelu(x):
    return jax.nn.gelu(x, approximate=True)

def _silu(x):
    return jax.nn.silu(x)

def _sigmoid(x):
    return jax.nn.sigmoid(x)

def _layernorm(x, axis=-1, eps=1e-05):
    m = jnp.mean(x, axis=axis, keepdims=True)
    v = jnp.var(x, axis=axis, keepdims=True)
    return (x - m) / jnp.sqrt(v + eps)

def _scatter_add(tgt, idx, src, axis=0):
    return tgt.at[idx].add(src)

def _segment_sum(src, seg, n):
    return jax.ops.segment_sum(src, seg, n)
kernel_name = 'mk_prb_d2_jaxref_r4_18b752'

def setup_inputs(seed: int=0):
    np.random.seed(seed)
    _w = jnp.asarray

    def _L0_attn_setup():
        import jax, jax.numpy as jnp
        import numpy as np
        DIM = 256
        N_HEADS = 16
        HEAD_DIM = DIM // N_HEADS
        D_LATENT = 64
        B, T = (1, 1024)
        key = jax.random.key(seed)
        ks = jax.random.split(key, 6)
        s = 0.02
        return {'x': jax.random.normal(ks[0], (B, T, DIM), dtype=jnp.float32), 'W_DKV': jax.random.normal(ks[1], (DIM, D_LATENT), dtype=jnp.float32) * s, 'W_UK': jax.random.normal(ks[2], (D_LATENT, DIM), dtype=jnp.float32) * s, 'W_UV': jax.random.normal(ks[3], (D_LATENT, DIM), dtype=jnp.float32) * s, 'W_UQ': jax.random.normal(ks[4], (DIM, DIM), dtype=jnp.float32) * s, 'W_O': jax.random.normal(ks[5], (DIM, DIM), dtype=jnp.float32) * s}
    _L0_attn_in = _L0_attn_setup()

    def _L0_ffn_setup():
        import jax, jax.numpy as jnp
        import numpy as np
        D_IN, D_HID = (256, 1024)

        def _ternary(key, shape):
            return jax.random.randint(key, shape, -1, 2).astype(jnp.float32)

        def _tlin(x, w, s):
            return jnp.einsum('bsi,oi->bso', x, w) * s
        key = jax.random.key(seed)
        ks = jax.random.split(key, 12)
        inv = lambda fan: 1.0 / np.sqrt(fan).astype(np.float32)
        return {'x': jax.random.normal(ks[0], (4, 512, D_IN), dtype=jnp.float32), 'w1_w': _ternary(ks[1], (D_HID, D_IN)), 'w1_s': jax.random.uniform(ks[2], (D_HID,), dtype=jnp.float32) * inv(D_IN), 'w2_w': _ternary(ks[3], (D_HID, D_IN)), 'w2_s': jax.random.uniform(ks[4], (D_HID,), dtype=jnp.float32) * inv(D_IN), 'h1_w': _ternary(ks[5], (D_HID, D_HID)), 'h1_s': jax.random.uniform(ks[6], (D_HID,), dtype=jnp.float32) * inv(D_HID), 'h2_w': _ternary(ks[7], (D_HID, D_HID)), 'h2_s': jax.random.uniform(ks[8], (D_HID,), dtype=jnp.float32) * inv(D_HID), 'w3_w': _ternary(ks[9], (D_IN, D_HID)), 'w3_s': jax.random.uniform(ks[10], (D_IN,), dtype=jnp.float32) * inv(D_HID)}
    _L0_ffn_in = _L0_ffn_setup()

    def _L1_attn_setup():
        import jax, jax.numpy as jnp
        import numpy as np
        DIM = 256
        HEADS = 16
        HEAD_DIM = DIM // HEADS
        NUM_FILTERS = 4
        NUM_TAPS = 101
        RES = 128

        def _fir_fft(c, sig):
            R = sig.shape[0]
            L = R + c.shape[0] - 1
            out = jnp.fft.ifft(jnp.fft.fft(sig, n=L) * jnp.fft.fft(c, n=L)).real
            return out[:R]
        key = jax.random.key(seed)
        ks = jax.random.split(key, 5)
        B, S = (2, 512)
        x = jax.random.normal(ks[0], (B, S, DIM), dtype=jnp.float32)
        Wqkv = jax.random.normal(ks[1], (3 * DIM, DIM), dtype=jnp.float32) * DIM ** (-0.5)
        Wout = jax.random.normal(ks[2], (DIM, DIM), dtype=jnp.float32) * DIM ** (-0.5)
        Wpos = jax.random.normal(ks[3], (HEADS, NUM_FILTERS), dtype=jnp.float32) * 0.5
        coeffs = jax.random.normal(ks[4], (NUM_FILTERS, NUM_TAPS), dtype=jnp.float32) * 0.05
        return {'x': x, 'Wqkv': Wqkv, 'Wout': Wout, 'Wpos': Wpos, 'coeffs': coeffs}
    _L1_attn_in = _L1_attn_setup()

    def _L1_ffn_setup():
        import jax, jax.numpy as jnp
        import numpy as np
        DM, NE, ES, ESZ = (256, 16, 4, 64)
        BATCH, SEQ = (8, 512)
        key = jax.random.key(seed)
        k = jax.random.split(key, 5)
        scale = 0.02
        return {'x': jax.random.normal(k[0], (BATCH, SEQ, DM), dtype=jnp.float32), 'controller': jax.random.normal(k[1], (DM, NE, ES), dtype=jnp.float32) * scale, 'f1': jax.random.normal(k[2], (DM, NE, ES, ESZ), dtype=jnp.float32) * scale, 'f2': jax.random.normal(k[3], (NE, ES, ESZ, DM), dtype=jnp.float32) * scale, 'bias': jax.random.normal(k[4], (NE, ES, ESZ), dtype=jnp.float32) * scale}
    _L1_ffn_in = _L1_ffn_setup()
    _d = {'L0_attn_x': _L0_attn_in['x'], 'L0_attn_W_DKV': _L0_attn_in['W_DKV'], 'L0_attn_W_UK': _L0_attn_in['W_UK'], 'L0_attn_W_UV': _L0_attn_in['W_UV'], 'L0_attn_W_UQ': _L0_attn_in['W_UQ'], 'L0_attn_W_O': _L0_attn_in['W_O'], 'L0_ffn_w1_w': _L0_ffn_in['w1_w'], 'L0_ffn_w1_s': _L0_ffn_in['w1_s'], 'L0_ffn_w2_w': _L0_ffn_in['w2_w'], 'L0_ffn_w2_s': _L0_ffn_in['w2_s'], 'L0_ffn_h1_w': _L0_ffn_in['h1_w'], 'L0_ffn_h1_s': _L0_ffn_in['h1_s'], 'L0_ffn_h2_w': _L0_ffn_in['h2_w'], 'L0_ffn_h2_s': _L0_ffn_in['h2_s'], 'L0_ffn_w3_w': _L0_ffn_in['w3_w'], 'L0_ffn_w3_s': _L0_ffn_in['w3_s'], 'L1_attn_Wqkv': _L1_attn_in['Wqkv'], 'L1_attn_Wout': _L1_attn_in['Wout'], 'L1_attn_Wpos': _L1_attn_in['Wpos'], 'L1_attn_coeffs': _L1_attn_in['coeffs'], 'L1_ffn_controller': _L1_ffn_in['controller'], 'L1_ffn_f1': _L1_ffn_in['f1'], 'L1_ffn_f2': _L1_ffn_in['f2'], 'L1_ffn_bias': _L1_ffn_in['bias']}
    _x0 = _d['L0_attn_x']
    _d['L0_attn_x'] = jax.random.normal(jax.random.fold_in(jax.random.key(seed), 1), (8, 512, 256), dtype=_x0.dtype)
    del _x0
    return _d

def reference(L0_attn_x, L0_attn_W_DKV, L0_attn_W_UK, L0_attn_W_UV, L0_attn_W_UQ, L0_attn_W_O, L0_ffn_w1_w, L0_ffn_w1_s, L0_ffn_w2_w, L0_ffn_w2_s, L0_ffn_h1_w, L0_ffn_h1_s, L0_ffn_h2_w, L0_ffn_h2_s, L0_ffn_w3_w, L0_ffn_w3_s, L1_attn_Wqkv, L1_attn_Wout, L1_attn_Wpos, L1_attn_coeffs, L1_ffn_controller, L1_ffn_f1, L1_ffn_f2, L1_ffn_bias):

    def _L0_attn_ref(x, W_DKV, W_UK, W_UV, W_UQ, W_O):
        import jax, jax.numpy as jnp
        import numpy as np
        DIM = 256
        N_HEADS = 16
        HEAD_DIM = DIM // N_HEADS
        D_LATENT = 64
        B, T = (1, 1024)
        b, t, d = x.shape
        h, hd = (N_HEADS, HEAD_DIM)
        c_kv = x @ W_DKV
        k = (c_kv @ W_UK).reshape(b, t, h, hd)
        v = (c_kv @ W_UV).reshape(b, t, h, hd)
        q = (x @ W_UQ).reshape(b, t, h, hd)
        scale = 1.0 / jnp.sqrt(jnp.asarray(hd, x.dtype))
        scores = jnp.einsum('bqhd,bkhd->bhqk', q, k) * scale
        causal = jnp.tril(jnp.ones((t, t), dtype=bool))
        scores = jnp.where(causal, scores, jnp.asarray(-jnp.inf, scores.dtype))
        probs = jax.nn.softmax(scores, axis=-1)
        ctx = jnp.einsum('bhqk,bkhd->bqhd', probs, v).reshape(b, t, d)
        return ctx @ W_O

    def _L0_ffn_ref(x, w1_w, w1_s, w2_w, w2_s, h1_w, h1_s, h2_w, h2_s, w3_w, w3_s):
        import jax, jax.numpy as jnp
        import numpy as np
        D_IN, D_HID = (256, 1024)

        def _ternary(key, shape):
            return jax.random.randint(key, shape, -1, 2).astype(jnp.float32)

        def _tlin(x, w, s):
            return jnp.einsum('bsi,oi->bso', x, w) * s
        h = jax.nn.silu(_tlin(x, w1_w, w1_s)) * _tlin(x, w2_w, w2_s)
        h = jax.nn.gelu(_tlin(h, h1_w, h1_s), approximate=False)
        h = jax.nn.gelu(_tlin(h, h2_w, h2_s), approximate=False)
        return _tlin(h, w3_w, w3_s)

    def _L1_attn_ref(x, Wqkv, Wout, Wpos, coeffs):
        import jax, jax.numpy as jnp
        import numpy as np
        DIM = 256
        HEADS = 16
        HEAD_DIM = DIM // HEADS
        NUM_FILTERS = 4
        NUM_TAPS = 101
        RES = 128

        def _fir_fft(c, sig):
            R = sig.shape[0]
            L = R + c.shape[0] - 1
            out = jnp.fft.ifft(jnp.fft.fft(sig, n=L) * jnp.fft.fft(c, n=L)).real
            return out[:R]
        B, S, D = x.shape
        scale = HEAD_DIM ** (-0.5)
        proto = jnp.linspace(0.0, 1.0, RES).astype(x.dtype)
        table = jax.vmap(_fir_fft, in_axes=(0, None))(coeffs, proto).T
        r = jnp.arange(S)
        rel = jnp.abs(r[None, :] - r[:, None]).astype(jnp.float32) / max(S - 1, 1)
        idx = jnp.clip(jnp.round(rel * (RES - 1)).astype(jnp.int32), 0, RES - 1)
        pos_feat = table[idx]
        pos_bias = jnp.einsum('ijf,hf->hij', pos_feat, Wpos)
        qkv = jnp.einsum('bsd,ed->bse', x, Wqkv)
        q, k, v = jnp.split(qkv, 3, axis=-1)
        q = q.reshape(B, S, HEADS, HEAD_DIM)
        k = k.reshape(B, S, HEADS, HEAD_DIM)
        v = v.reshape(B, S, HEADS, HEAD_DIM)
        logits = jnp.einsum('bihd,bjhd->bhij', q, k) * scale + pos_bias[None]
        attn = jax.nn.softmax(logits, axis=-1)
        out = jnp.einsum('bhij,bjhd->bihd', attn, v).reshape(B, S, D)
        return jnp.einsum('bsd,ed->bse', out, Wout)

    def _L1_ffn_ref(x, controller, f1, f2, bias):
        import jax, jax.numpy as jnp
        import numpy as np
        DM, NE, ES, ESZ = (256, 16, 4, 64)
        BATCH, SEQ = (8, 512)
        ne = controller.shape[1]
        d = x.shape[-1]
        grouped = x.reshape(x.shape[:-2] + (-1, ne, d))
        logits = jnp.einsum('...btd,des->...btes', grouped, controller)
        tie = jnp.linspace(0.0, 1e-06, ne, dtype=logits.dtype).reshape(ne, 1, 1)
        logits = logits + tie
        perm = (logits == jnp.max(logits, axis=-3, keepdims=True)).astype(x.dtype)
        sel = jnp.einsum('...btd,...btes->...besd', grouped, perm)
        inner = jax.nn.relu(jnp.einsum('...besd,desf->...besf', sel, f1) + bias)
        inter = jnp.einsum('...besf,esfd->...besd', inner, f2)
        out = jnp.einsum('...besd,...btes->...btd', inter, perm)
        return out.reshape(x.shape)
    x = L0_attn_x
    xn = _layernorm(x, axis=-1)
    x = x + _L0_attn_ref(xn, L0_attn_W_DKV, L0_attn_W_UK, L0_attn_W_UV, L0_attn_W_UQ, L0_attn_W_O) + _L0_ffn_ref(xn, L0_ffn_w1_w, L0_ffn_w1_s, L0_ffn_w2_w, L0_ffn_w2_s, L0_ffn_h1_w, L0_ffn_h1_s, L0_ffn_h2_w, L0_ffn_h2_s, L0_ffn_w3_w, L0_ffn_w3_s)
    xn = _layernorm(x, axis=-1)
    x = x + _L1_attn_ref(xn, L1_attn_Wqkv, L1_attn_Wout, L1_attn_Wpos, L1_attn_coeffs) + _L1_ffn_ref(xn, L1_ffn_controller, L1_ffn_f1, L1_ffn_f2, L1_ffn_bias)
    return x

_drawn_inputs = setup_inputs


def setup_inputs(seed=0):
    import zlib

    import numpy as np

    out = dict(_drawn_inputs(seed))
    spreads = {}
    factors = {}
    for name, (base, spread) in spreads.items():
        noise = np.random.default_rng([zlib.crc32(name.encode()), seed]).standard_normal(out[name].shape)
        drawn = base * np.exp(spread * noise) if base else spread * noise
        out[name] = jnp.asarray(drawn.astype(out[name].dtype))
    for name, factor in factors.items():
        out[name] = (out[name] * factor).astype(out[name].dtype)
    return out
```

```python
from contextlib import ExitStack

import numpy as np

import concourse.bass as bass
from concourse import mybir

F32 = mybir.dt.float32
F32R = mybir.dt.float32r
ALU = mybir.AluOpType
ACT = mybir.ActivationFunctionType
AX_X = mybir.AxisListType.X

P = 128
B, T, D = 8, 512, 256
KD = D // P
TT = T // P
H, HD = 16, 16
PAIRS = H // 2
QUADS = H // 4
HROWS = P // 2
LATENT = 64
HID = 1024
KH = HID // P
NE, ES, ESZ = 16, 4, 64
E = NE * ES
GROUPS = B * T // NE
RES, TAPS = 128, 101
NEG = -1.0e30
MIN_N = 256
PARTS = ((0, 1), (1, 0), (0, 0))
EPS = 1.0e-5
UW = 2 * T - P
UOFF = T - P


class Tally:

    def __init__(self, sem, per=0, grant=0, unit=1):
        self.sem, self.per, self.grant, self.unit = sem, per * unit, grant * unit, unit

    def at(self, k, i=0):
        return i * self.per + (self.grant + k * self.unit)


def consts():
    row = np.arange(P) % HROWS
    cols = np.zeros((P, 4), np.float32)
    cols[(row // HD) == 1, 0] = -1.0
    cols[(row // HD) == 2, 1] = -1.0
    cols[row == 3 * HD, 1] = 1.0
    cols[row == 3 * HD, 2] = -1.0
    cols[LATENT:, 3] = -1.0
    mask = np.zeros((P, T), np.float32)
    mask[:, T - P:] = np.where(np.arange(P)[None, :] <= np.arange(P)[:, None], 0.0, NEG)
    ramp = np.linspace(0.0, 1.0, RES).astype(np.float32)
    dist = np.abs(np.arange(2 * T) - (T - 1)).astype(np.float32) / np.float32(T - 1)
    idx = np.clip(np.round(dist * np.float32(RES - 1)).astype(np.int32), 0, RES - 1)
    n = idx[None, :] - np.arange(TAPS)[:, None]
    fir = np.where(n >= 0, ramp[np.clip(n, 0, RES - 1)], 0.0).astype(np.float32)
    step = np.arange(NE, dtype=np.float32) / np.float32(NE - 1)
    tie = np.tile(np.float32(1e-6) * step, (P, T // NE)).astype(np.float32)
    group = (np.arange(P)[:, None] // NE == np.arange(P // NE)[None, :]).astype(np.float32)
    odd = (np.arange(T)[None, :] // NE % 2 == np.arange(P)[:, None] // E).astype(np.float32)
    return {"c_parity": odd, "c_flip": np.ascontiguousarray(np.eye(P, dtype=np.float32)[::-1]), "c_ident": np.eye(P, dtype=np.float32), "c_cols": cols, "c_mask": mask, "c_fir": fir,
            "c_tie": tie, "c_group": group, "c_pow": np.full((P, TT), -0.5, np.float32)}


def clear(nc, tallies):
    with nc.Block() as block:
        @block.sync
        def _(sp):
            for tally in tallies:
                sp.sem_clear(tally.sem)


def attention(nc, tag, layer, x_d, out_d, xh_d, xl_d, xn_d, w, c):
    causal = layer == 0
    with ExitStack() as ctx:
        def sb(name, shape, dt=F32):
            return ctx.enter_context(nc.sbuf_tensor(f"{tag}_{name}", shape, dt))

        tallies = []

        def sem(name, per=0, grant=0, unit=1):
            tallies.append(Tally(ctx.enter_context(nc.semaphore(f"{tag}_{name}")), per, grant, unit))
            return tallies[-1]

        ident, cols = sb("ident", [P, P]), sb("cols", [P, 4])
        power = sb("power", [P, TT])
        q_low, k_low, k_one, c_low = (cols[:, j:j + 1] for j in range(4))
        wq = sb("wq", [P, 2, KD, PAIRS, P], F32R)
        KK = 1 if causal else KD
        wk = sb("wk", [P, 2, KK, PAIRS, P], F32R)
        wv = sb("wv", [P, 2, KK, D], F32R)
        wo = sb("wo", [P, KD, D])
        if causal:
            wc = sb("wc", [P, 2, KD, P], F32R)
            mask = sb("mask", [P, T])
        else:
            bias = sb("bias", [P, H, UW])
        x_in, xn = sb("x_in", [P, TT, D]), sb("xn", [P, TT, D])
        stats, moments = sb("stats", [P, TT, 6]), sb("moments", [P, TT, 2])
        var_eps, rstd = sb("var_eps", [P, TT]), sb("rstd", [P, TT])
        xh, xl = sb("xh", [P, KD, T], F32R), sb("xl", [P, KD, T], F32R)
        cs = sb("cs", [P, T], F32R) if causal else None
        top = sb("top", [P, 2, T], F32R)
        qs, ks = sb("qs", [P, QUADS, 2, T], F32R), sb("ks", [P, QUADS, 2, 2, T], F32R)
        vals_sb = sb("vals", [P, TT * H * (HD + 1) + 32])
        vals = vals_sb[:, 0:TT * H * (HD + 1)].rearrange("p (t h d) -> p t h d", t=TT, h=H)
        peak = sb("peak", [P, TT, 2, P])
        prob = sb("prob", [P, 4, 2, T])
        o_sb = sb("o_sb", [P, T])
        inv = sb("inv", [P, QUADS, TT, 4])
        mix, mixt = sb("mix", [P, TT, D]), sb("mixt", [P, KD, T])
        out_sb = sb("out_sb", [P, TT, D])

        banks = [ctx.enter_context(nc.psum_tensor(f"{tag}_ps{j}", [P, T], F32)) for j in range(8)]
        a_bank, b_bank, m_bank, o_bank, misc = banks[0:2], banks[2:4], banks[4], banks[5], banks[6:8]

        consts_in = sem("consts_in", unit=16)
        w_in = sem("w_in", unit=16)
        w_hi, w_ready, zeroed = sem("w_hi"), sem("w_ready"), sem("zeroed")
        x_loaded = sem("x_loaded", 1, unit=16)
        x_saved = sem("x_saved", 2 if causal else 3, unit=16)
        out_saved = sem("out_saved", 1, grant=1, unit=16)
        stats_done, moments_done = sem("stats_done", TT), sem("moments_done", TT)
        eps_done, rstd_ready, xn_ready = sem("eps_done", 1), sem("rstd_ready", 1), sem("xn_ready", TT)
        xt_ps, xh_ready, xl_ready = sem("xt_ps", KD), sem("xh_ready", KD), sem("xl_ready", KD)
        c_ps, c_top, c_ready = sem("c_ps", 1), sem("c_top", 1), sem("c_ready", 1)
        v_ps, v_ready = sem("v_ps", 2), sem("v_ready", 2)
        s_ps, s_top, s_ready = (sem(n, 2 * PAIRS) for n in ("s_ps", "s_top", "s_ready"))
        a_ps, a_max = sem("a_ps", 4 * H), sem("a_max", 4 * H)
        m_ps, qm_ready = sem("m_ps", PAIRS), sem("qm_ready", PAIRS)
        b_ps, p_exp, p_done = sem("b_ps", 4 * H), sem("p_exp", 4 * H), sem("p_done", 4 * H)
        pv_ps, o_copied, ot_ps = sem("pv_ps", QUADS), sem("o_copied", QUADS), sem("ot_ps", QUADS)
        inv_ready, mix_ready = sem("inv_ready", QUADS), sem("mix_ready", QUADS)
        mt_ps, mixt_ready = sem("mt_ps", KD), sem("mixt_ready", KD)
        out_ps, out_ready = sem("out_ps", 2), sem("out_ready", 2)

        flip = o_sb[:, 0:P]
        rising = [prob[:, a].rearrange("p j t -> p (j t)")[:, 0:UW] for a in range(4)]
        rising_in = [sem(f"rising_in{a}", unit=16) for a in range(4)] if not causal else None
        bias_ps, bias_ready = sem("bias_ps"), sem("bias_ready")

        p_add = [sem(f"p_add{m}", 2 * H) for m in range(2)]
        p_copied = sem("p_copied", 2 * H)
        held_dve, held_pool = sem("held_dve"), sem("held_pool")

        with nc.sbuf_tensor(f"{tag}_stage", [P, KD, D], F32) as stage_w, \
             nc.sbuf_tensor(f"{tag}_hi", [P, KD, D], F32R) as hi_w, nc.Block() as block:
            @block.sync
            def _(sp):
                sp.dma_start(ident[:], c["c_ident"]).then_inc(consts_in.sem, 16)
                sp.dma_start(cols[:], c["c_cols"]).then_inc(consts_in.sem, 16)
                sp.dma_start(power[:], c["c_pow"]).then_inc(consts_in.sem, 16)
                sp.dma_start(wo[:], w["wo"].rearrange("(k p) n -> p k n", p=P)).then_inc(consts_in.sem, 16)
                if causal:
                    sp.dma_start(mask[:], c["c_mask"]).then_inc(consts_in.sem, 16)
                else:
                    sp.dma_start(flip, c["c_flip"]).then_inc(consts_in.sem, 16)
                for n, (name, ap, rows) in enumerate(w["loads"]):
                    if n:
                        sp.wait_ge(w_ready.sem, n)
                    for dst, src in w["place"](name, stage_w, ap):
                        sp.dma_start(dst, src).then_inc(w_in.sem, 16)
                sp.wait_ge(consts_in.sem, 16 * 5)
                if causal:
                    return
                for h in range(H):
                    if h >= 4:
                        sp.wait_ge(bias_ps.sem, 2 * (h - 3))
                    src = bass.AP(w["ext"].tensor, w["ext"].offset + h * 2 * T, [[1, P], [1, UW]])
                    sp.dma_start(rising[h % 4], src).then_inc(rising_in[h % 4].sem, 16)

            if not causal:
                @block.tensor
                def _(pe):
                    pe.wait_ge(consts_in.sem, 16 * 5)
                    for n in range(2 * H):
                        h, half = n // 2, n % 2
                        pe.wait_ge(rising_in[h % 4].sem, 16 * (h // 4 + 1))
                        if n >= 8:
                            pe.wait_ge(bias_ready.sem, n - 7)
                        pe.matmul(banks[n % 8][:, 0:UW // 2], flip, rising[h % 4][:, half * (UW // 2):(half + 1) * (UW // 2)],
                                  start=True, stop=True).then_inc(bias_ps.sem, 1)

                @block.scalar
                def _(act):
                    for n in range(2 * H):
                        h, half = n // 2, n % 2
                        act.wait_ge(bias_ps.sem, n + 1)
                        act.activation(bias[:, h, half * (UW // 2):(half + 1) * (UW // 2)], banks[n % 8][:, 0:UW // 2],
                                       ACT.Copy).then_inc(bias_ready.sem, 1)

            @block.vector
            def _(dve):
                dve.memset(wq[:].bitcast(F32), 0.0).then_inc(zeroed.sem, 1)
                dve.memset(wk[:].bitcast(F32), 0.0).then_inc(zeroed.sem, 1)
                dve.memset(vals_sb[:], 0.0).then_inc(zeroed.sem, 1)
                dve.memset(peak[:], 0.0).then_inc(zeroed.sem, 1)
                dve.memset(ks[:].bitcast(F32), 0.0).then_inc(zeroed.sem, 1)
                dve.wait_ge(zeroed.sem, 5)
                dve.memset(vals[:, :, :, HD:HD + 1], 1.0).then_inc(zeroed.sem, 1)
                loaded = 0
                for n, (name, ap, rows) in enumerate(w["loads"]):
                    loaded += 16 * len(w["place"](name, stage_w, ap))
                    kk = 1 if (causal and name in "kv") else KD
                    cols_n = LATENT if name == "c" else D
                    scale = HD ** -0.5 if name == "k" else 1.0
                    raw = stage_w[:, 0:kk, 0:cols_n]
                    hi = hi_w[:, 0:kk, 0:cols_n]
                    dve.wait_ge(w_in.sem, loaded)
                    dve.tensor_copy(hi, raw).then_inc(w_hi.sem, 1)
                    dve.wait_ge(w_hi.sem, n * 2 + 1)
                    dve.tensor_tensor(raw, raw, hi.bitcast(F32), ALU.subtract).then_inc(w_hi.sem, 1)
                    dve.wait_ge(w_hi.sem, n * 2 + 2)
                    for part, src in ((0, hi.bitcast(F32)), (1, raw)):
                        if name in "qk":
                            dst = wq if name == "q" else wk
                            for slot in range(3):
                                for k in range(kk):
                                    o = dst[:, part, k].rearrange("p g (a s d) -> p (g a) s d", a=2, s=4)
                                    last = dve.tensor_scalar(
                                        o[:, :, slot, :], src[:, k].rearrange("p (h d) -> p h d", d=HD),
                                        scale, None, ALU.mult)
                        elif name == "v":
                            last = dve.tensor_copy(wv[:, part], src)
                        else:
                            for twice in range(2):
                                last = dve.tensor_copy(
                                    wc[:, part, :, twice * LATENT:(twice + 1) * LATENT], src)
                    last.then_inc(w_ready.sem, 1)
                    dve.wait_ge(w_ready.sem, n + 1)

        SLOTS = 4 * TT + 2
        STEADY = []
        LAG = 1 if causal else 2
        for s in range(QUADS):
            now, before, before2 = (0, s), ((0, s - 1) if s else (-1, QUADS - 1)), ((0, s - 2) if s > 1 else (-1, s + 2))
            after = (0, s + 1) if s + 1 < QUADS else (1, 0)
            for slot in range(SLOTS):
                if slot < 16:
                    STEADY.append(("score", 0, 16 * s + slot))
                if slot == 1:
                    STEADY.append(("maxima", before[0], 2 * before[1] + 1))
                if slot == 11:
                    STEADY.append(("maxima", 0, 2 * s))
                if slot == 3:
                    STEADY.append(("value", before2[0], TT * before2[1] + TT - 1))
                if slot in (9, 13, 17):
                    STEADY.append(("value", before[0], TT * before[1] + (9, 13, 17).index(slot)))
                if slot >= 2:
                    STEADY.append(("prob", before[0], 16 * before[1] + slot - 2))
                n = slot - 2 - LAG
                if n >= 0:
                    STEADY.append(("prob_exp", before[0], 16 * before[1] + n))
                elif n + SLOTS < 16:
                    STEADY.append(("prob_exp", before2[0], 16 * before2[1] + n + SLOTS))
                for kind, at in (("stack", (3, 7, 11, 14)), ("stack_top", (4, 8, 12, 15)), ("stack_low", (5, 9, 13, 16))):
                    if slot in at:
                        STEADY.append((kind, after[0], 4 * after[1] + at.index(slot)))
                if slot == 4:
                    STEADY.append(("heads_copy", before2[0], before2[1]))
                if slot == 6:
                    STEADY.append(("heads_turn", before2[0], before2[1]))
                if slot == 8:
                    STEADY.append(("heads_norm", before2[0], before2[1]))
                STEADY += {(1, 5): [("v", 0, 0), ("v", 0, 1)],
                           (1, 10): [("mix_turn", -1, 0), ("mix_turn", -1, 1), ("ln_stats", 1, 0)],
                           (1, 13): [("out", -1, 0), ("out", -1, 1)],
                           (1, 15): [("store", -1, 0)],
                           (2, 6): [("ln", 1, 0)],
                           (2, 16): [("x_turn", 1, 0), ("x_turn", 1, 1)],
                           (2, 17): [("x_high", 1, 0), ("x_high", 1, 1)],
                           (3, 0): [("x_low", 1, 0), ("x_low", 1, 1)],
                           (3, 1): [("latent", 1, 0)] * causal,
                           (3, 2): [("latent_top", 1, 0)] * causal,
                           (3, 3): [("latent_low", 1, 0)] * causal}.get((s, slot), [])

        LAST_READ = {"stack": s_ready, "heads_turn": mix_ready, "v": v_ready, "mix_turn": mixt_ready,
                     "out": out_ready, "x_turn": xl_ready}
        USES = [e for e in STEADY if e[0] in LAST_READ]
        assert len(USES) % 2 == 0

        def bank(kind, n):
            return misc[[(u[0], u[2]) for u in USES].index((kind, n)) % 2]

        def there(b):
            return not isinstance(b, int) or 0 <= b < B

        def turns(eng, emit):
            def turn(i):
                for kind, off, n in STEADY:
                    if there(i + off):
                        emit(kind, i + off, n, i)
            turn(-1)
            turn(0)
            with eng.Fori(1, B - 1) as i:
                turn(i)
            turn(B - 1)
            turn(B)

        def wait(eng, tally, k, b):
            value = tally.at(k, b)
            if not isinstance(value, int) or value > 0:
                eng.wait_ge(tally.sem, value)

        def hold(eng, held, tally, k, b):
            wait(eng, tally, k, b)
            if not isinstance(b, int):
                eng.sem_inc(held.sem, 1)

        def keys_of(n):
            j, a = n % 16 // 4, n % 4
            wide = max(T - j * P, MIN_N) if causal else T
            return n // 16, j, a, wide, T - wide

        def add_bias(eng, b, n, src):
            g, j, a, wide, q0 = keys_of(n)
            eng.tensor_tensor(prob[:, a, j % 2], src, bias[:, 4 * g + a, UOFF - j * P:UOFF - j * P + T],
                              ALU.add).then_inc(p_add[n % 2].sem, 1)

        with nc.Block() as block:
            @block.sync
            def _(sp):
                saves = 2 if causal else 3

                def load(b):
                    sp.dma_start(x_in[:], x_d[b].rearrange("(t p) d -> p t d", p=P)).then_inc(x_loaded.sem, 16)

                def save(b):
                    wait(sp, xh_ready, KD, b)
                    sp.dma_start(xh_d[b], xh[:].bitcast(F32)).then_inc(x_saved.sem, 16)
                    wait(sp, xl_ready, KD, b)
                    sp.dma_start(xl_d[b], xl[:].bitcast(F32)).then_inc(x_saved.sem, 16)
                    if not causal:
                        sp.dma_start(xn_d[b], xn[:]).then_inc(x_saved.sem, 16)
                    wait(sp, x_saved, saves, b)

                load(0)
                with sp.Fori(0, B - 1) as i:
                    save(i)
                    load(i + 1)
                save(B - 1)

            @block.gpsimd
            def _(pool):
                def emit(kind, b, n, i):
                    if kind == "ln_stats":
                        wait(pool, eps_done, 1, b)
                        nc.gpsimd.tensor_tensor(rstd[:], var_eps[:], power[:], ALU.pow).then_inc(rstd_ready.sem, 1)
                    if kind == "prob" and causal:
                        g, j, a, wide, q0 = keys_of(n)
                        hold(pool, held_pool, p_exp, n + 1, b)
                        blk = prob[:, a, j % 2, j * P:(j + 1) * P]
                        nc.gpsimd.affine_select(out=blk, in_=blk, compare_op=ALU.is_ge, fill=0.0, base=0,
                                                pattern=[[1, P]], channel_multiplier=-1).then_inc(p_done.sem, 1)
                    if kind == "prob" and not causal and n % 2:
                        g, j, a, wide, q0 = keys_of(n)
                        wait(pool, p_copied, n // 2 + 1, b)
                        add_bias(pool, b, n, prob[:, a, j % 2])
                turns(pool, emit)

            @block.scalar
            def _(act):
                act.sem_inc(out_saved.sem, 16)

                def emit(kind, b, n, i):
                    if kind == "x_high":
                        wait(act, xt_ps, n + 1, b)
                        act.copy(xh[:, n], bank("x_turn", n)[:]).then_inc(xh_ready.sem, 1)
                    if kind == "latent_top":
                        wait(act, c_ps, 1, b)
                        act.copy(top[:, 0], m_bank[:]).then_inc(c_top.sem, 1)
                    if kind == "v":
                        wait(act, v_ps, n + 1, b)
                        act.copy(vals[:, 2 * n:2 * n + 2, :, 0:HD],
                                 bank("v", n)[:].rearrange("p (t h d) -> p t h d", t=2, d=HD)).then_inc(v_ready.sem, 1)
                    if kind == "stack_top":
                        wait(act, s_ps, n + 1, b)
                        if causal and n == 0:
                            wait(act, c_ready, 1, b)
                        wait(act, s_ready, n - 1, b)
                        src = bank("stack", n)[:]
                        if n % 2 == 0:
                            act.activation(top[:, 0], src, ACT.Copy).then_inc(s_top.sem, 1)
                        else:
                            act.activation(top[:, 1], src, ACT.Identity, bias=k_one).then_inc(s_top.sem, 1)
                    if kind == "prob_exp" and causal:
                        g, j, a, wide, q0 = keys_of(n)
                        wait(act, b_ps, n + 1, b)
                        act.activation(prob[:, a, j % 2, j * P:T], b_bank[n % 2][:, j * P - q0:wide],
                                       ACT.Exp).then_inc(p_exp.sem, 1)
                    if kind == "prob" and not causal and n % 2:
                        g, j, a, wide, q0 = keys_of(n)
                        wait(act, b_ps, n + 1, b)
                        act.activation(prob[:, a, j % 2], b_bank[1][:], ACT.Copy).then_inc(p_copied.sem, 1)
                    if kind == "prob_exp" and not causal:
                        g, j, a, wide, q0 = keys_of(n)
                        wait(act, p_add[n % 2], n // 2 + 1, b)
                        act.activation(prob[:, a, j % 2], prob[:, a, j % 2], ACT.Exp).then_inc(p_done.sem, 1)
                    if kind == "heads_copy":
                        wait(act, pv_ps, n + 1, b)
                        act.copy(o_sb[:], o_bank[:]).then_inc(o_copied.sem, 1)
                    if kind == "mix_turn":
                        wait(act, mt_ps, n + 1, b)
                        act.copy(mixt[:, n], bank(kind, n)[:]).then_inc(mixt_ready.sem, 1)
                    if kind == "out":
                        if n == 0:
                            wait(act, out_saved, 1, b - 1)
                        wait(act, out_ps, n + 1, b)
                        act.copy(out_sb[:, 2 * n:2 * n + 2],
                                 bank(kind, n)[:].rearrange("p (t d) -> p t d", t=2)).then_inc(out_ready.sem, 1)
                    if kind == "store":
                        wait(act, out_ready, 2, b)
                        act.dma_start(out_d[b].rearrange("(t p) d -> p t d", p=P), out_sb[:]).then_inc(out_saved.sem, 16)
                turns(act, emit)
                act.wait_ge(out_saved.sem, out_saved.at(1, B - 1))

            @block.vector
            def _(dve):
                def emit(kind, b, n, i):
                    if kind == "ln_stats":
                        wait(dve, x_loaded, 1, b)
                        for t in range(TT):
                            dve.bn_stats(stats[:, t], x_in[:, t]).then_inc(stats_done.sem, 1)
                        for t in range(TT):
                            hold(dve, held_dve, stats_done, t + 1, b)
                            dve.bn_aggr(moments[:, t], stats[:, t]).then_inc(moments_done.sem, 1)
                        wait(dve, moments_done, TT, b)
                        dve.tensor_scalar(var_eps[:], moments[:, :, 1], EPS, None, ALU.add).then_inc(eps_done.sem, 1)
                    if kind == "ln":
                        wait(dve, rstd_ready, 1, b)
                        for t in range(TT):
                            dve.tensor_scalar(xn[:, t], x_in[:, t], moments[:, t, 0:1], rstd[:, t:t + 1],
                                              ALU.subtract, ALU.mult).then_inc(xn_ready.sem, 1)
                    if kind == "x_low":
                        wait(dve, xh_ready, n + 1, b)
                        dve.tensor_tensor(xl[:, n], bank("x_turn", n)[:], xh[:, n].bitcast(F32),
                                          ALU.subtract).then_inc(xl_ready.sem, 1)
                    if kind == "latent_low":
                        wait(dve, c_top, 1, b)
                        dve.scalar_tensor_tensor(cs[:], top[:, 0].bitcast(F32), c_low, m_bank[:],
                                                 ALU.mult, ALU.add).then_inc(c_ready.sem, 1)
                    if kind == "stack_low":
                        wait(dve, s_top, n + 1, b)
                        g, pr, src = n // 4, n // 2 % 2, bank("stack", n)
                        if n % 2 == 0:
                            dve.scalar_tensor_tensor(qs[:, g, pr], top[:, 0].bitcast(F32), q_low, src[:],
                                                     ALU.mult, ALU.add).then_inc(s_ready.sem, 1)
                        else:
                            for a in range(2):
                                r = slice(a * HROWS, (a + 1) * HROWS)
                                ins = dve.scalar_tensor_tensor(ks[r, g, pr, a], top[r, 1].bitcast(F32), k_low[r],
                                                               src[r, :], ALU.mult, ALU.add)
                            ins.then_inc(s_ready.sem, 1)
                    if kind == "maxima":
                        g, pr = n // 2, n % 2
                        wait(dve, m_ps, n + 1, b)
                        dve.tensor_tensor(qs[:, g, pr], m_bank[:], qs[:, g, pr].bitcast(F32), ALU.add)\
                           .then_inc(qm_ready.sem, 1)
                    if kind == "score":
                        pr, t, a = n // 8 % 2, n // 2 % 4, n % 2
                        wide = (t + 1) * P if causal else T
                        add = mask[:, T - wide:T] if causal else \
                            bias[:, 4 * (n // 16) + 2 * pr + a, UOFF - t * P:UOFF - t * P + T]
                        src = a_bank[n % 2][:, 0:wide]
                        col = a * HROWS + 3 * HD
                        hold(dve, held_dve, a_ps, n + 1, b)
                        dve.tensor_tensor_reduce(src, src, add, 1.0, 3 * NEG, ALU.add, ALU.max,
                                                 peak[:, t, pr, col:col + 1]).then_inc(a_max.sem, 1)
                    if kind == "prob" and not causal and n % 2 == 0:
                        wait(dve, b_ps, n + 1, b)
                        add_bias(dve, b, n, b_bank[0][:])
                    if kind == "heads_norm":
                        wait(dve, ot_ps, n + 1, b)
                        src = bank("heads_turn", n)[:].rearrange("p (t a d) -> p t a d", t=TT, a=4)
                        dve.reciprocal(inv[:, n], src[:, :, :, HD]).then_inc(inv_ready.sem, 1)
                        wait(dve, inv_ready, n + 1, b)
                        dst = mix[:].rearrange("p t (g a d) -> p t g a d", g=QUADS, a=4)[:, :, n]
                        dve.tensor_tensor(dst, src[:, :, :, 0:HD], inv[:, n].unsqueeze(3).to_broadcast([P, TT, 4, HD]),
                                          ALU.mult).then_inc(mix_ready.sem, 1)
                turns(dve, emit)

            @block.tensor
            def _(pe):
                def claim(kind, n, i):
                    names = [(u[0], u[2]) for u in USES]
                    at = names.index((kind, n))
                    for m in range(at - 2, at - len(USES) - 1, -2):
                        before, off, k = USES[m]
                        bb = i + off - (1 if m < 0 else 0)
                        if there(bb):
                            wait(pe, LAST_READ[before], k + 1, bb)
                            break
                    return misc[at % 2]

                def product(out, pairs):
                    for m, (left, right) in enumerate(pairs):
                        ins = pe.matmul(out, left, right, start=(m == 0), stop=(m == len(pairs) - 1))
                    return ins

                def emit(kind, b, n, i):
                    if kind == "x_turn":
                        out = claim(kind, n, i)
                        wait(pe, xn_ready, TT, b)
                        for t in range(TT):
                            ins = pe.transpose(out[:, t * P:(t + 1) * P], xn[:, t, n * P:(n + 1) * P], ident[:])
                        ins.then_inc(xt_ps.sem, 1)
                    if kind == "latent":
                        wait(pe, qm_ready, PAIRS - 2, b - 1)
                        wait(pe, xl_ready, KD, b)
                        product(m_bank[:], [(wc[:, p, k], (xl if q else xh)[:, k]) for k in range(KD)
                                            for p, q in PARTS]).then_inc(c_ps.sem, 1)
                    if kind == "v":
                        out = claim(kind, n, i)
                        wait(pe, c_ready if causal else xl_ready, 1 if causal else KD, b)
                        for t in range(2 * n, 2 * n + 2):
                            o = out[:, (t % 2) * D:(t % 2 + 1) * D]
                            cut = slice(t * P, (t + 1) * P)
                            if causal:
                                ins = product(o, [(cs[:, cut], wv[:, p, 0]) for p in (1, 0)])
                            else:
                                ins = product(o, [((xl if q else xh)[:, k, cut], wv[:, p, k]) for k in range(KD)
                                                  for p, q in PARTS])
                        ins.then_inc(v_ps.sem, 1)
                    if kind == "stack":
                        out = claim(kind, n, i)
                        if n % 2 and causal:
                            wait(pe, c_ready, 1, b)
                            pairs = [(wk[:, p, 0, n // 2], cs[:]) for p in (1, 0)]
                        else:
                            wait(pe, xl_ready, KD, b)
                            pairs = [((wk if n % 2 else wq)[:, p, k, n // 2], (xl if q else xh)[:, k])
                                     for k in range(KD) for p, q in PARTS]
                        product(out[:], pairs).then_inc(s_ps.sem, 1)
                    if kind == "score":
                        g, pr, t, a = n // 16, n // 8 % 2, n // 2 % 4, n % 2
                        if n % 16 in (0, 8):
                            wait(pe, s_ready, 4 * g + 2 * pr + 2, b)
                        wait(pe, a_max, n - 1, b)
                        wide = max((t + 1) * P, MIN_N) if causal else T
                        pe.matmul(a_bank[n % 2][:, 0:wide], qs[:, g, pr, t * P:(t + 1) * P],
                                  ks[:, g, pr, a, 0:wide], start=True, stop=True).then_inc(a_ps.sem, 1)
                    if kind == "maxima":
                        g, pr = n // 2, n % 2
                        wait(pe, a_max, 16 * g + 8 * pr + 8, b)
                        wait(pe, qm_ready, n, b)
                        if causal and n == 0:
                            wait(pe, c_ready, 1, b)
                        for t in range(TT):
                            ins = pe.transpose(m_bank[:, t * P:(t + 1) * P], peak[:, t, pr], ident[:])
                        ins.then_inc(m_ps.sem, 1)
                    if kind == "prob":
                        g, j, a, wide, q0 = keys_of(n)
                        if n % 16 == 0:
                            wait(pe, qm_ready, 2 * g + 1, b)
                        if n % 16 == 2:
                            wait(pe, qm_ready, 2 * g + 2, b)
                        if causal:
                            wait(pe, p_exp, n - 1, b)
                        else:
                            wait(pe, p_copied if n % 2 else p_add[0], n // 2, b)
                        pe.matmul(b_bank[n % 2][:, 0:wide], ks[:, g, a // 2, a % 2, j * P:(j + 1) * P],
                                  qs[:, g, a // 2, q0:T], start=True, stop=True).then_inc(b_ps.sem, 1)
                    if kind == "value":
                        g, j = n // TT, n % TT
                        if j == 0:
                            wait(pe, o_copied, g, b)
                        if n == 0:
                            wait(pe, v_ready, 2, b)
                        wait(pe, p_done, 16 * g + 4 * j + 4, b)
                        q0 = j * P if causal else 0
                        for a in range(4):
                            v0 = (j * H + 4 * g + a) * (HD + 1)
                            ins = pe.matmul(o_bank[32 * a:32 * a + 32, q0:T], vals_sb[:, v0:v0 + 32],
                                            prob[:, a, j % 2, q0:T], start=(j == 0), stop=(j == TT - 1),
                                            skip_group_check=True)
                        if j == TT - 1:
                            ins.then_inc(pv_ps.sem, 1)
                    if kind == "heads_turn":
                        out = claim(kind, n, i)
                        wait(pe, o_copied, n + 1, b)
                        for t in range(TT):
                            ins = pe.transpose(out[:, t * P:(t + 1) * P], o_sb[:, t * P:(t + 1) * P], ident[:])
                        ins.then_inc(ot_ps.sem, 1)
                    if kind == "mix_turn":
                        out = claim(kind, n, i)
                        wait(pe, mix_ready, QUADS, b)
                        for t in range(TT):
                            ins = pe.transpose(out[:, t * P:(t + 1) * P], mix[:, t, n * P:(n + 1) * P], ident[:])
                        ins.then_inc(mt_ps.sem, 1)
                    if kind == "out":
                        out = claim(kind, n, i)
                        wait(pe, mixt_ready, KD, b)
                        for t in range(2 * n, 2 * n + 2):
                            ins = product(out[:, (t % 2) * D:(t % 2 + 1) * D],
                                          [(mixt[:, k, t * P:(t + 1) * P], wo[:, k]) for k in range(KD)])
                        ins.then_inc(out_ps.sem, 1)
                turns(pe, emit)
        clear(nc, tallies)



def ffn(nc, x_d, attn_d, xh_d, xl_d, out_d, w, c, lo_d):
    with ExitStack() as ctx:
        def sb(name, shape, dt=F32):
            return ctx.enter_context(nc.sbuf_tensor(f"f_{name}", shape, dt))

        tallies = []

        def sem(name, per=0, grant=0, unit=1):
            tallies.append(Tally(ctx.enter_context(nc.semaphore(f"f_{name}")), per, grant, unit))
            return tallies[-1]

        names = ("w1", "w2", "h1", "h2", "w3")
        wide = {"w1": HID, "w2": HID, "h1": HID, "h2": HID, "w3": D}
        deep = {"w1": KD, "w2": KD, "h1": KH, "h2": KH, "w3": KH}
        hi = {m: sb(f"hi_{m}", [P, deep[m], wide[m]], F32R) for m in names}
        gate_s, both_s, h1_s, h2_s = (sb(n, [P, KH]) for n in ("gate_s", "both_s", "h1_s", "h2_s"))
        out_s = sb("out_s", [P, D])
        ident = sb("ident", [P, P])
        flag = sb("flag", [1, 1], mybir.dt.int32)
        low = sb("low", [P, 2, KH, P], F32R)
        psum = [ctx.enter_context(nc.psum_tensor(f"f_ps{j}", [P, T], F32)) for j in range(8)]

        loaded = [sem(f"loaded{j}", unit=16) for j in range(2)]
        saved = [sem(f"saved{j}", unit=16) for j in range(2)]
        hi_done, lo_done = sem("hi_done"), sem("lo_done")
        s_in, s_done, peak_ps, peak_done = sem("s_in", unit=16), sem("s_done"), sem("peak_ps"), sem("peak_done")

        CH = 1024
        chunks = [(m, k, o) for m in names for k in range(deep[m]) for o in range(0, wide[m], CH)]
        with nc.sbuf_tensor("f_raw", [P, 2, CH], F32) as raw, nc.sbuf_tensor("f_lo", [P, 2, CH], F32) as lo, \
             nc.sbuf_tensor("f_junk", [P, CH], F32) as junk, \
             nc.sbuf_tensor("f_peaks", [P, 2, len(chunks)], F32) as peaks, \
             nc.sbuf_tensor("f_peak", [P, 1], F32) as peak, nc.sbuf_tensor("f_any", [1, 1], F32) as top, \
             nc.Block() as block:
            @block.sync
            def _(sp):
                sp.dma_start(ident[:], c["c_ident"]).then_inc(s_in.sem, 16)
                for dst, src in ((gate_s, "w1_s"), (both_s, "w2_s"), (h1_s, "h1_s"), (h2_s, "h2_s")):
                    sp.dma_start(dst[:], w[src]).then_inc(s_in.sem, 16)
                s3 = w["w3_s"]
                sp.dma_start(out_s[:], bass.AP(s3.tensor, s3.offset, [[0, P], [1, D]])).then_inc(s_in.sem, 16)
                for n, (m, k, o) in enumerate(chunks):
                    cut = min(CH, wide[m])
                    if n >= 2:
                        sp.wait_ge(lo_done.sem, n - 1)
                    sp.dma_start(raw[:, n % 2, 0:cut], w[m + "_w"][k * P:(k + 1) * P, o:o + cut])\
                      .then_inc(loaded[n % 2].sem, 16)

            @block.scalar
            def _(act):
                for n, (m, k, o) in enumerate(chunks):
                    cut = min(CH, wide[m])
                    act.wait_ge(lo_done.sem, n + 1)
                    act.dma_start(lo_d[m][k * P:(k + 1) * P, o:o + cut], lo[:, n % 2, 0:cut])\
                       .then_inc(saved[n % 2].sem, 16)
                for j in range(2):
                    act.wait_ge(saved[j].sem, 16 * (len(chunks) // 2))

            @block.vector
            def _(dve):
                for n, (m, k, o) in enumerate(chunks):
                    cut = min(CH, wide[m])
                    h = hi[m][:, k, o:o + cut]
                    dve.wait_ge(loaded[n % 2].sem, 16 * (n // 2 + 1))
                    if n >= 2:
                        dve.wait_ge(saved[n % 2].sem, 16 * (n // 2))
                    dve.tensor_copy(h, raw[:, n % 2, 0:cut]).then_inc(hi_done.sem, 1)
                    dve.wait_ge(hi_done.sem, n + 1)
                    if n:
                        dve.wait_ge(lo_done.sem, n)
                    dve.tensor_tensor_reduce(junk[:, 0:cut], h.bitcast(F32), raw[:, n % 2, 0:cut], 1.0, 0.0, ALU.subtract,
                                             ALU.max, peaks[:, 0, n:n + 1])
                    dve.tensor_tensor_reduce(lo[:, n % 2, 0:cut], raw[:, n % 2, 0:cut], h.bitcast(F32), 1.0, 0.0,
                                             ALU.subtract, ALU.max, peaks[:, 1, n:n + 1]).then_inc(lo_done.sem, 1)
                dve.wait_ge(lo_done.sem, len(chunks))
                dve.tensor_reduce(peak[:], peaks[:].rearrange("p a n -> p (a n)"), AX_X, ALU.max).then_inc(peak_done.sem, 1)
                dve.wait_ge(peak_ps.sem, 1)
                dve.tensor_reduce(top[:], psum[0][0:1, 0:P], AX_X, ALU.max).then_inc(peak_done.sem, 1)
                dve.wait_ge(peak_done.sem, 2)
                dve.tensor_scalar(flag[:], top[:], 0.0, None, ALU.is_gt)
                dve.wait_ge(s_in.sem, 16 * 6)
                dve.tensor_scalar(gate_s[:], gate_s[:], 0.5, None, ALU.mult).then_inc(s_done.sem, 1)
                dve.wait_ge(s_done.sem, 1)
                dve.tensor_tensor(both_s[:], gate_s[:], both_s[:], ALU.mult).then_inc(s_done.sem, 1)
                dve.wait_ge(s_done.sem, 2)

            @block.tensor
            def _(pe):
                pe.wait_ge(s_in.sem, 16 * 6)
                pe.wait_ge(peak_done.sem, 1)
                pe.transpose(psum[0][0:1, 0:P], peak[:], ident[:]).then_inc(peak_ps.sem, 1)

        xh, xl = sb("xh", [P, KD, T], F32R), sb("xl", [P, KD, T], F32R)
        x_in, attn = sb("x_in", [P, TT, D]), sb("attn", [P, TT, D])
        out_sb = sb("out_sb", [P, TT, D])
        tanh = sb("tanh", [P, 2, T])
        gated = sb("gated", [P, 2, T])
        full = sb("full", [P, 2, T])
        hh = [sb(f"hh{j}", [P, KH, T], F32R) for j in range(2)]
        hl = [sb(f"hl{j}", [P, KH, T], F32R) for j in range(2)]

        xt_in, x_in_s = sem("xt_in", 2, unit=16), sem("x_in_s", 2, unit=16)
        gu_ps, t_done, gate_done = sem("gu_ps", KH), sem("t_done", KH), sem("gate_done", KH)
        h_full, h_hi, h_lo = sem("h_full", 2 * KH), sem("h_hi", 3 * KH), sem("h_lo", 3 * KH)
        h_ps, o_ps = sem("h_ps", 2 * KH), sem("o_ps", 2)
        scaled, added, out_done = sem("scaled", 2), sem("added", 1), sem("out_done", 2)
        out_saved = sem("out_saved", 1, grant=1, unit=16)
        lo_in = [sem("lo_in0", 2 * KH + 1, unit=16), sem("lo_in1", 2 * KH, unit=16)]
        lo_used = sem("lo_used", 4 * KH + 1, grant=1)
        half_gated = sem("half_gated", KH)

        gates, ups, hidden, outs = psum[0:2], psum[2:4], psum[4:6], psum[6:8]
        low_w3 = low[:].rearrange("p s k n -> p (s k n)").rearrange("p (k n) -> p k n", k=KH)
        STREAM = [(m, o) for o in range(KH) for m in ("w1", "w2")] + [("h1", o) for o in range(KH)] + \
                 [("h2", o) for o in range(KH)] + [("w3", 0)]

        with nc.Block() as block:
            @block.sync
            def _(sp):
                any_low = sp.value_load(flag[0:1, 0:1], min_val=0, max_val=1)

                def load(b):
                    sp.dma_start(xh[:].bitcast(F32), xh_d[b]).then_inc(xt_in.sem, 16)
                    sp.dma_start(xl[:].bitcast(F32), xl_d[b]).then_inc(xt_in.sem, 16)

                def load_sums(b):
                    sp.dma_start(x_in[:], x_d[b].rearrange("(t p) d -> p t d", p=P)).then_inc(x_in_s.sem, 16)
                    sp.dma_start(attn[:], attn_d[b].rearrange("(t p) d -> p t d", p=P)).then_inc(x_in_s.sem, 16)

                def batch(b):
                    load_sums(b)
                    with sp.If(any_low == 1):
                        for n, (m, o) in enumerate(STREAM):
                            sp.wait_ge(lo_used.sem, lo_used.at(n if m == "w3" else max(n - 1, 0), b))
                            src = lo_d[m].rearrange("(k p) n -> p k n", p=P)
                            if m == "w3":
                                dst = low_w3.bitcast(F32)
                            else:
                                dst, src = low[:, n % 2, 0:deep[m]].bitcast(F32), src[:, :, o * P:(o + 1) * P]
                            sp.dma_start(dst, src).then_inc(lo_in[n % 2].sem, 16)

                def store(b):
                    sp.wait_ge(out_done.sem, out_done.at(2, b))
                    sp.dma_start(out_d[b].rearrange("(t p) d -> p t d", p=P), out_sb[:]).then_inc(out_saved.sem, 16)

                load(0)
                with sp.Fori(0, B - 1) as i:
                    batch(i)
                    sp.wait_ge(gu_ps.sem, gu_ps.at(KH, i))
                    load(i + 1)
                    store(i)
                batch(B - 1)
                store(B - 1)
                sp.wait_ge(out_saved.sem, out_saved.at(1, B - 1))

            @block.gpsimd
            def _(pool):
                with pool.Fori(0, B) as i:
                    pool.wait_ge(x_in_s.sem, x_in_s.at(2, i))
                    pool.tensor_tensor(x_in[:], x_in[:], attn[:], ALU.add).then_inc(added.sem, 1)
                    for n in range(3 * KH):
                        layer, o = n // KH, n % KH
                        pool.wait_ge(h_hi.sem, h_hi.at(n + 1, i))
                        pool.tensor_tensor(hl[layer % 2][:, o], full[:, n % 2], hh[layer % 2][:, o].bitcast(F32),
                                           ALU.subtract).then_inc(h_lo.sem, 1)

            @block.scalar
            def _(act):
                with act.Fori(0, B) as i:
                    for o in range(KH):
                        act.wait_ge(gu_ps.sem, gu_ps.at(o + 1, i))
                        if o >= 2:
                            act.wait_ge(gate_done.sem, gate_done.at(o - 1, i))
                        act.activation(tanh[:, o % 2], gates[o % 2][:], ACT.Tanh, scale=gate_s[:, o:o + 1])\
                           .then_inc(t_done.sem, 1)
                    for n in range(KH, 3 * KH):
                        layer, o = n // KH, n % KH
                        act.wait_ge(h_ps.sem, h_ps.at(n - KH + 1, i))
                        act.wait_ge(h_lo.sem, h_lo.at(n - 1, i))
                        act.activation(full[:, n % 2], hidden[n % 2][:], ACT.Gelu,
                                       scale=(h1_s if layer == 1 else h2_s)[:, o:o + 1]).then_inc(h_full.sem, 1)

            @block.vector
            def _(dve):
                dve.sem_inc(lo_used.sem, 1)
                dve.sem_inc(out_saved.sem, 16)
                with dve.Fori(0, B) as i:
                    for n in range(3 * KH):
                        layer, o = n // KH, n % KH
                        if layer == 0:
                            dve.wait_ge(t_done.sem, t_done.at(o + 1, i))
                            dve.scalar_tensor_tensor(gated[:, o % 2], tanh[:, o % 2], 1.0, gates[o % 2][:],
                                                     ALU.add, ALU.mult).then_inc(half_gated.sem, 1)
                            dve.wait_ge(half_gated.sem, half_gated.at(o + 1, i))
                            if o >= 2:
                                dve.wait_ge(h_lo.sem, h_lo.at(o - 1, i))
                            dve.scalar_tensor_tensor(full[:, o % 2], ups[o % 2][:], both_s[:, o:o + 1], gated[:, o % 2],
                                                     ALU.mult, ALU.mult).then_inc(gate_done.sem, 1)
                            dve.wait_ge(gate_done.sem, gate_done.at(o + 1, i))
                        else:
                            dve.wait_ge(h_full.sem, h_full.at(n - KH + 1, i))
                        dve.tensor_copy(hh[layer % 2][:, o], full[:, n % 2]).then_inc(h_hi.sem, 1)
                    dve.wait_ge(out_saved.sem, out_saved.at(0, i))
                    for m in range(2):
                        dve.wait_ge(o_ps.sem, o_ps.at(m + 1, i))
                        dst = out_sb[:, 2 * m:2 * m + 2]
                        dve.tensor_tensor(dst, outs[m][:].rearrange("p (t d) -> p t d", t=2),
                                          out_s[:].unsqueeze(1).to_broadcast([P, 2, D]), ALU.mult).then_inc(scaled.sem, 1)
                        dve.wait_ge(added.sem, added.at(1, i))
                        dve.wait_ge(scaled.sem, scaled.at(m + 1, i))
                        dve.tensor_tensor(dst, x_in[:, 2 * m:2 * m + 2], dst, ALU.add).then_inc(out_done.sem, 1)

            @block.tensor
            def _(pe):
                any_low = pe.value_load(flag[0:1, 0:1], min_val=0, max_val=1)

                def products(outs_, pairs, first, last):
                    for k in range(len(pairs[0])):
                        for out, ps in zip(outs_, pairs):
                            ins = pe.matmul(out, *ps[k], start=first and k == 0, stop=last and k == len(ps) - 1,
                                            skip_group_check=True)
                    return ins

                with pe.Fori(0, B) as i:
                    pe.wait_ge(xt_in.sem, xt_in.at(2, i))
                    for o in range(KH):
                        cut = slice(o * P, (o + 1) * P)
                        if o >= 2:
                            pe.wait_ge(gate_done.sem, gate_done.at(o - 1, i))
                        two = [gates[o % 2][:], ups[o % 2][:]]
                        products(two, [[(hi[m][:, k, cut], xl[:, k]) for k in range(KD)] for m in ("w1", "w2")], True, False)
                        with pe.If(any_low == 1):
                            for s in range(2):
                                pe.wait_ge(lo_in[s].sem, lo_in[s].at(o + 1, i))
                            products(two, [[(low[:, s, k], xh[:, k]) for k in range(KD)] for s in range(2)],
                                     False, False).then_inc(lo_used.sem, 2)
                        products(two, [[(hi[m][:, k, cut], xh[:, k]) for k in range(KD)] for m in ("w1", "w2")],
                                 False, True).then_inc(gu_ps.sem, 1)
                    for n in range(2 * KH):
                        layer, o = n // KH, n % KH
                        m, cut = ("h1", "h2")[layer], slice(o * P, (o + 1) * P)
                        high, lo_ = hh[layer % 2], hl[layer % 2]
                        if n >= 2:
                            pe.wait_ge(h_full.sem, h_full.at(n - 1, i))
                        out = hidden[n % 2][:]
                        for part, src, done in ((0, high, h_hi), (1, lo_, h_lo)):
                            for k in range(KH):
                                if o == 0:
                                    pe.wait_ge(done.sem, done.at(layer * KH + k + 1, i))
                                ins = pe.matmul(out, hi[m][:, k, cut], src[:, k], start=(part == 0 and k == 0),
                                                stop=(part == 1 and k == KH - 1), skip_group_check=True)
                            if part == 0:
                                with pe.If(any_low == 1):
                                    u = 2 * KH + n
                                    pe.wait_ge(lo_in[u % 2].sem, lo_in[u % 2].at(u // 2 + 1, i))
                                    products([out], [[(low[:, u % 2, k], high[:, k]) for k in range(KH)]],
                                             False, False).then_inc(lo_used.sem, 1)
                        ins.then_inc(h_ps.sem, 1)
                    high, lo_ = hh[0], hl[0]
                    for t in range(TT):
                        cut = slice(t * P, (t + 1) * P)
                        out = outs[t // 2][:, (t % 2) * D:(t % 2 + 1) * D]
                        for part, src, done in ((0, high, h_hi), (1, lo_, h_lo)):
                            for k in range(KH):
                                if t == 0:
                                    pe.wait_ge(done.sem, done.at(2 * KH + k + 1, i))
                                ins = pe.matmul(out, src[:, k, cut], hi["w3"][:, k], start=(part == 0 and k == 0),
                                                stop=(part == 1 and k == KH - 1), skip_group_check=True)
                            if part == 0:
                                with pe.If(any_low == 1):
                                    pe.wait_ge(lo_in[0].sem, lo_in[0].at(2 * KH + 1, i))
                                    last = products([out], [[(high[:, k, cut], low_w3[:, k]) for k in range(KH)]],
                                                    False, False)
                                    if t == TT - 1:
                                        last.then_inc(lo_used.sem, 1)
                        if t % 2:
                            ins.then_inc(o_ps.sem, 1)
        clear(nc, tallies)


def bias_table(nc, wpos, coeffs, ext_d, c):
    with nc.sbuf_tensor("t_wpos", list(wpos.shape), F32) as wpos_sb, nc.sbuf_tensor("t_coeffs", list(coeffs.shape), F32) as co_sb, \
         nc.sbuf_tensor("t_fir", [TAPS, 2 * T], F32) as fir, nc.sbuf_tensor("t_cw", [TAPS, H], F32) as cw, \
         nc.sbuf_tensor("t_ext", [H, 2, T], F32) as ext, nc.psum_tensor("t_ps0", [P, T], F32) as ps0, \
         nc.psum_tensor("t_ps1", [P, T], F32) as ps1, nc.semaphore("t_in") as loaded, nc.semaphore("t_cw_ps") as cw_ps, \
         nc.semaphore("t_cw_ready") as cw_ready, nc.semaphore("t_ext_ps") as ext_ps, \
         nc.semaphore("t_ext_ready") as ext_ready, nc.semaphore("t_saved") as saved, nc.Block() as block:
        @block.sync
        def _(sp):
            sp.dma_start(wpos_sb[:], wpos).then_inc(loaded, 16)
            sp.dma_start(co_sb[:], coeffs).then_inc(loaded, 16)
            sp.dma_start(fir[:], c["c_fir"]).then_inc(loaded, 16)
            sp.wait_ge(ext_ready, 2)
            sp.dma_start(ext_d, ext[:].rearrange("h a t -> h (a t)")).then_inc(saved, 16)
            sp.wait_ge(saved, 16)

        @block.tensor
        def _(pe):
            pe.wait_ge(loaded, 16 * 3)
            pe.matmul(ps0[0:TAPS, 0:H], co_sb[:], wpos_sb[:], start=True, stop=True).then_inc(cw_ps, 1)
            pe.wait_ge(cw_ready, 1)
            for n, ps in enumerate((ps0, ps1)):
                pe.matmul(ps[0:H, :], cw[:], fir[:, n * T:(n + 1) * T], start=True, stop=True).then_inc(ext_ps, 1)

        @block.vector
        def _(dve):
            dve.wait_ge(cw_ps, 1)
            dve.tensor_copy(cw[:], ps0[0:TAPS, 0:H]).then_inc(cw_ready, 1)
            for n, ps in enumerate((ps0, ps1)):
                dve.wait_ge(ext_ps, n + 1)
                dve.tensor_copy(ext[:, n], ps[0:H, :]).then_inc(ext_ready, 1)


def skewed(eng, front, back):
    front(0, 0)
    for s in range(2):
        front(s + 1, (s + 1) % 2)
        back(s, s)
    with eng.Fori(1, B // 2 - 1) as i:
        for s in range(2):
            front(i * 2 + (s + 1), (s + 1) % 2)
            back(i * 2 + s, s)
    front(B - 1, 1)
    back(B - 2, 0)
    back(B - 1, 1)


def select(nc, sel, xh_d, xl_d, xn_d, pt_d, controller, c):
    with ExitStack() as ctx:
        def sb(name, shape, dt=F32):
            return ctx.enter_context(nc.sbuf_tensor(f"s_{name}", shape, dt))

        tallies = []

        def sem(name, per=0, grant=0, unit=1):
            tallies.append(Tally(ctx.enter_context(nc.semaphore(f"s_{name}")), per, grant, unit))
            return tallies[-1]

        G = P // NE
        ident, tie, parity, group = sb("ident", [P, P]), sb("tie", [P, T]), sb("parity", [P, T]), sb("group", [P, G])
        w_raw, w_low = sb("w_raw", [P, KD, P]), sb("w_low", [P, KD, P], F32R)
        w_high = sb("w_high", [P, KD, P], F32R)
        xh, xl = sb("xh", [P, 2, KD, T], F32R), sb("xl", [P, 2, KD, T], F32R)
        xn = sb("xn", [P, 2, TT, D])
        th, tl = sb("th", [P, 2, TT, D], F32R), sb("tl", [P, 2, TT, D], F32R)
        logits, best = sb("logits", [P, T]), sb("best", [P, T // NE])
        perm, picks = sb("perm", [P, 2, T]), sb("picks", [P, 2, T])
        blocks = sb("blocks", [P, TT, G, E], F32R)
        banks = [ctx.enter_context(nc.psum_tensor(f"s_ps{j}", [P, T], F32)) for j in range(8)]
        lg_bank, tr_bank, sel_banks = banks[0], banks[1], banks[2:6]

        consts_in, w_hi, w_ready = sem("consts_in", unit=16), sem("w_hi"), sem("w_ready")
        xt_in = [sem(f"xt_in{s}", 2, unit=16) for s in range(2)]
        xn_in = [sem(f"xn_in{s}", 1, unit=16) for s in range(2)]
        pt_saved = [sem(f"pt_saved{s}", 1, unit=16) for s in range(2)]
        th_ready, tl_ready = sem("th_ready", 1), sem("tl_ready", 1)
        lg_ps, lg_ready, best_ready = sem("lg_ps", 1), sem("lg_ready", 1), sem("best_ready", 1)
        perm_ready, pt_ready = sem("perm_ready", 1), sem("pt_ready", 1)
        tr_ps, blocks_ready = sem("tr_ps", 1), sem("blocks_ready", TT)
        sel_ps = sem("sel_ps", 2 * TT)
        sel_done = [sem("sel_done0", TT), sem("sel_done1", TT)]

        def wait(eng, tally, k, b):
            value = tally.at(k, b)
            if not isinstance(value, int) or value > 0:
                eng.wait_ge(tally.sem, value)

        def slot_wait(eng, tally, k, b, s):
            if isinstance(b, int):
                if tally.at(k, b // 2) > 0:
                    eng.wait_ge(tally.sem, tally.at(k, b // 2))
            else:
                eng.wait_ge(tally.sem, b * (tally.per // 2) + (tally.at(k) - s * (tally.per // 2)))

        with nc.Block() as block:
            @block.sync
            def _(sp):
                for dst, src in ((ident, "c_ident"), (tie, "c_tie"), (parity, "c_parity"), (group, "c_group")):
                    sp.dma_start(dst[:], c[src]).then_inc(consts_in.sem, 16)
                for twice in range(2):
                    sp.dma_start(w_raw[:, :, twice * E:(twice + 1) * E],
                                 controller.rearrange("(k p) n -> p k n", p=P)).then_inc(consts_in.sem, 16)

                def front(b, s):
                    wait(sp, lg_ps, -1, b)
                    sp.dma_start(xh[:, s].bitcast(F32), xh_d[b]).then_inc(xt_in[s].sem, 16)
                    sp.dma_start(xl[:, s].bitcast(F32), xl_d[b]).then_inc(xt_in[s].sem, 16)
                    wait(sp, tl_ready, -1, b)
                    sp.dma_start(xn[:, s], xn_d[b]).then_inc(xn_in[s].sem, 16)

                def back(b, s):
                    wait(sp, pt_ready, 1, b)
                    sp.dma_start(pt_d[b], picks[:, s]).then_inc(pt_saved[s].sem, 16)
                skewed(sp, front, back)
                for s in range(2):
                    sp.wait_ge(pt_saved[s].sem, pt_saved[s].at(1, B // 2 - 1))

            @block.gpsimd
            def _(pool):
                def front(b, s):
                    slot_wait(pool, xn_in[s], 1, b, s)
                    wait(pool, th_ready, 1, b)
                    wait(pool, sel_ps, 2 * TT, b - 2)
                    pool.tensor_tensor(tl[:, s], xn[:, s], th[:, s].bitcast(F32), ALU.subtract).then_inc(tl_ready.sem, 1)
                skewed(pool, front, lambda b, s: None)

            @block.scalar
            def _(act):
                def front(b, s):
                    slot_wait(act, xn_in[s], 1, b, s)
                    wait(act, sel_ps, 2 * TT, b - 2)
                    act.activation(th[:, s], xn[:, s], ACT.Copy).then_inc(th_ready.sem, 1)

                def back(b, s):
                    for t in range(TT):
                        n = 2 * t + 1
                        wait(act, sel_ps, n + 1, b)
                        act.activation(sel[:, 1, :, bass.ds(b * (TT * G) + t * G, G)],
                                       sel_banks[n % 4][:].rearrange("p (g e) -> p e g", g=G), ACT.Copy)\
                           .then_inc(sel_done[1].sem, 1)
                skewed(act, front, back)

            @block.vector
            def _(dve):
                dve.wait_ge(consts_in.sem, 16 * 6)
                dve.tensor_copy(w_high[:], w_raw[:]).then_inc(w_hi.sem, 1)
                dve.wait_ge(w_hi.sem, 1)
                dve.tensor_tensor(w_low[:], w_raw[:], w_high[:].bitcast(F32), ALU.subtract).then_inc(w_ready.sem, 1)

                def front(b, s):
                    wait(dve, best_ready, 0, b)
                    wait(dve, perm_ready, 0, b)
                    wait(dve, lg_ps, 1, b)
                    dve.tensor_tensor(logits[:], lg_bank[:], tie[:], ALU.add).then_inc(lg_ready.sem, 1)
                    wait(dve, lg_ready, 1, b)
                    grouped = logits[:].rearrange("p (g j) -> p g j", j=NE)
                    dve.tensor_reduce(best[:], grouped, AX_X, ALU.max).then_inc(best_ready.sem, 1)
                    wait(dve, best_ready, 1, b)
                    wait(dve, tr_ps, 1, b - 2)
                    dve.tensor_tensor(perm[:, s].rearrange("p (g j) -> p g j", j=NE), grouped,
                                      best[:].unsqueeze(2).to_broadcast([P, T // NE, NE]), ALU.is_equal)\
                       .then_inc(perm_ready.sem, 1)
                    wait(dve, perm_ready, 1, b)
                    if not isinstance(b, int) or b >= 2:
                        slot_wait(dve, pt_saved[s], 0, b, s)
                    dve.tensor_tensor(picks[:, s], perm[:, s], parity[:], ALU.mult).then_inc(pt_ready.sem, 1)

                def back(b, s):
                    wait(dve, tr_ps, 1, b)
                    wait(dve, sel_ps, 2 * TT, b - 1)
                    for t in range(TT):
                        dve.tensor_tensor(blocks[:, t], tr_bank[:, t * P:t * P + E].unsqueeze(1).to_broadcast([P, G, E]),
                                          group[:].unsqueeze(2).to_broadcast([P, G, E]), ALU.mult)\
                           .then_inc(blocks_ready.sem, 1)
                    for t in range(TT):
                        n = 2 * t
                        wait(dve, sel_ps, n + 1, b)
                        dve.tensor_copy(sel[:, 0, :, bass.ds(b * (TT * G) + t * G, G)],
                                        sel_banks[n % 4][:].rearrange("p (g e) -> p e g", g=G))\
                           .then_inc(sel_done[0].sem, 1)
                skewed(dve, front, back)

            @block.tensor
            def _(pe):
                pe.wait_ge(w_ready.sem, 1)

                def front(b, s):
                    slot_wait(pe, xt_in[s], 2, b, s)
                    wait(pe, lg_ready, 0, b)
                    pairs = [(w, x[:, s, k]) for k in range(KD) for w, x in
                             ((w_high[:, k], xl), (w_low[:, k], xh), (w_high[:, k], xh))]
                    for m, (left, right) in enumerate(pairs):
                        ins = pe.matmul(lg_bank[:], left, right, start=m == 0, stop=m == len(pairs) - 1)
                    ins.then_inc(lg_ps.sem, 1)

                def back(b, s):
                    wait(pe, perm_ready, 1, b)
                    wait(pe, blocks_ready, 0, b)
                    for t in range(TT):
                        ins = pe.transpose(tr_bank[:, t * P:(t + 1) * P], perm[:, s, t * P:(t + 1) * P], ident[:])
                    ins.then_inc(tr_ps.sem, 1)
                    wait(pe, tl_ready, 1, b)
                    for n in range(2 * TT):
                        t, half = n // 2, n % 2
                        wait(pe, sel_done[half], t - 1, b)
                        wait(pe, blocks_ready, t + 1, b)
                        cut = slice(half * P, (half + 1) * P)
                        rhs = blocks[:, t].rearrange("p g e -> p (g e)")
                        out = sel_banks[n % 4][:]
                        pe.matmul(out, tl[:, s, t, cut], rhs, start=True, stop=False)
                        pe.matmul(out, th[:, s, t, cut], rhs, start=False, stop=True).then_inc(sel_ps.sem, 1)
                skewed(pe, front, back)


def experts(nc, sel, inter_d, f1, f2, bias, c):
    with ExitStack() as ctx:
        def sb(name, shape, dt=F32):
            return ctx.enter_context(nc.sbuf_tensor(f"e_{name}", shape, dt))

        tallies = []

        def sem(name, per=0, grant=0, unit=1):
            tallies.append(Tally(ctx.enter_context(nc.semaphore(f"e_{name}")), per, grant, unit))
            return tallies[-1]

        def slots(name, per):
            return [sem(f"{name}{s}", per, unit=16) for s in range(2)]

        R, GH, TURNS = 2, GROUPS // P, E // 4
        w1, w2 = sb("w1", [P, 2, KD, R * P]), sb("w2", [P, 2, R, 2, D])
        bias_sb = sb("bias", [ESZ, E])
        inner = sb("inner", [P, 2, GROUPS])
        stage = sb("stage", [P, 2, GH, R, 2 * D])
        banks = [ctx.enter_context(nc.psum_tensor(f"e_ps{j}", [P, T], F32)) for j in range(8)]
        in_banks, out_banks = banks[0:2], banks[4:8]

        bias_in, zeroed = sem("bias_in", unit=16), sem("zeroed")
        w1_in, w2_in, saved = slots("w1_in", 1), slots("w2_in", 2), slots("saved", GH)
        in_ps, inner_ready = sem("in_ps", R), sem("inner_ready", 2 * R)
        out_ps = sem("out_ps", GH * R)
        staged = [sem("staged0", R), sem("staged1", R)]

        def at(tally, k, i, s, back=0):
            return i * (2 * tally.per) + ((s - back) * tally.per + k * tally.unit)

        def wait(eng, tally, value):
            if not isinstance(value, int) or value > 0:
                eng.wait_ge(tally.sem, value)

        def loop(eng, body):
            for s in range(2):
                body(0, s)
            with eng.Fori(1, TURNS // 2) as i:
                for s in range(2):
                    body(i, s)

        with nc.Block() as block:
            @block.sync
            def _(sp):
                sp.dma_start(bias_sb[:], bias).then_inc(bias_in.sem, 16)
                sp.wait_ge(zeroed.sem, 1)

                def body(i, s):
                    m = i * 2 + s
                    wait(sp, in_ps, at(in_ps, R, i, s, 2))
                    sp.dma_start(w1[:, s], f1[:, bass.ds(m * (R * P), R * P)].rearrange("(k p) n -> p k n", p=P))\
                      .then_inc(w1_in[s].sem, 16)
                    wait(sp, out_ps, at(out_ps, GH * R, i, s, 2))
                    src = f2[bass.ds(m * (R * P), R * P)].rearrange("(j a f) d -> a f j d", a=2, f=ESZ)
                    for a in range(2):
                        sp.dma_start(w2[a * ESZ:(a + 1) * ESZ, s, :, a], src[a]).then_inc(w2_in[s].sem, 16)
                loop(sp, body)

            @block.gpsimd
            def _(pool):
                def body(i, s):
                    m = i * 2 + s
                    for gh in range(GH):
                        wait(pool, staged[gh], at(staged[gh], R, i, s))
                        pool.dma_start(inter_d[gh * P:(gh + 1) * P, bass.ds(m * (2 * R), 2 * R)],
                                       stage[:, s, gh].rearrange("p j (a d) -> p (j a) d", a=2)).then_inc(saved[s].sem, 16)
                loop(pool, body)
                for s in range(2):
                    pool.wait_ge(saved[s].sem, saved[s].at(GH, TURNS // 2 - 1))

            @block.scalar
            def _(act):
                act.wait_ge(bias_in.sem, 16)

                def body(i, s):
                    m = i * 2 + s
                    for j in range(R):
                        wait(act, in_ps, at(in_ps, j + 1, i, s))
                        wait(act, out_ps, at(out_ps, GH * (j - 1), i, s))
                        for a in range(2):
                            act.activation(inner[a * ESZ:(a + 1) * ESZ, j % 2],
                                           in_banks[j % 2][0:ESZ, a * GROUPS:(a + 1) * GROUPS], ACT.Relu,
                                           bias=bias_sb[:, bass.ds(m * (2 * R) + (2 * j + a), 1)]).then_inc(inner_ready.sem, 1)
                        if j == 0:
                            wait(act, saved[s], saved[s].at(0, i))
                        wait(act, out_ps, at(out_ps, GH * j + 1, i, s))
                        act.activation(stage[:, s, 0, j], out_banks[j % 2 * 2][:], ACT.Copy).then_inc(staged[0].sem, 1)
                loop(act, body)

            @block.vector
            def _(dve):
                dve.memset(w2[:], 0.0).then_inc(zeroed.sem, 1)

                def body(i, s):
                    for j in range(R):
                        if j == 0:
                            wait(dve, saved[s], saved[s].at(0, i))
                        wait(dve, out_ps, at(out_ps, GH * j + 2, i, s))
                        dve.tensor_copy(stage[:, s, 1, j], out_banks[j % 2 * 2 + 1][:]).then_inc(staged[1].sem, 1)
                loop(dve, body)

            @block.tensor
            def _(pe):
                def body(i, s):
                    m = i * 2 + s
                    for j in range(R):
                        if j == 0:
                            wait(pe, w1_in[s], w1_in[s].at(1, i))
                        wait(pe, inner_ready, at(inner_ready, 2 * (j - 1), i, s))
                        for a in range(2):
                            for k in range(KD):
                                ins = pe.matmul(in_banks[j % 2][0:ESZ, a * GROUPS:(a + 1) * GROUPS],
                                                w1[:, s, k, j * P + a * ESZ:j * P + (a + 1) * ESZ],
                                                sel[:, k, bass.ds(m * (2 * R) + (2 * j + a), 1), :].rearrange("p a g -> p (a g)"),
                                                start=k == 0, stop=k == KD - 1, skip_group_check=True)
                        ins.then_inc(in_ps.sem, 1)
                        if j == 0:
                            wait(pe, w2_in[s], w2_in[s].at(2, i))
                        wait(pe, inner_ready, at(inner_ready, 2 * (j + 1), i, s))
                        for gh in range(GH):
                            wait(pe, staged[gh], at(staged[gh], j - 1, i, s))
                            pe.matmul(out_banks[j % 2 * 2 + gh][:], inner[:, j % 2, gh * P:(gh + 1) * P],
                                      w2[:, s, j].rearrange("p a d -> p (a d)"), start=True, stop=True)\
                              .then_inc(out_ps.sem, 1)
                loop(pe, body)


def combine(nc, inter_d, pt_d, x_d, attn_d, out_d):
    with ExitStack() as ctx:
        def sb(name, shape, dt=F32):
            return ctx.enter_context(nc.sbuf_tensor(f"c_{name}", shape, dt))

        tallies = []

        def sem(name, per=0, grant=0, unit=1):
            tallies.append(Tally(ctx.enter_context(nc.semaphore(f"c_{name}")), per, grant, unit))
            return tallies[-1]

        C = 4
        rows = sb("rows", [P, TT, C, D])
        picks, x_in, attn = sb("picks", [P, 2, T]), sb("x_in", [P, 2, TT, D]), sb("attn", [P, 2, TT, D])
        out_sb = sb("out_sb", [P, 2, TT, D])
        banks = [ctx.enter_context(nc.psum_tensor(f"c_ps{j}", [P, T], F32)) for j in range(TT)]
        rows_in = [sem(f"rows_in{t}", 1, unit=16) for t in range(TT)]
        in_s = [sem(f"in{s}", 3, unit=16) for s in range(2)]
        added, moe_ps, summed = sem("added", 1), sem("moe_ps", TT), sem("summed", TT)
        saved = [sem(f"saved{s}", 1, unit=16) for s in range(2)]

        def at(tally, k, i, s, back=0):
            return i * (2 * tally.per) + ((s - back) * tally.per + k * tally.unit)

        def wait(eng, tally, value):
            if not isinstance(value, int) or value > 0:
                eng.wait_ge(tally.sem, value)

        def loop(eng, body):
            for s in range(2):
                body(0, s)
            with eng.Fori(1, B // 2) as i:
                for s in range(2):
                    body(i, s)

        with nc.Block() as block:
            @block.sync
            def _(sp):
                def body(i, s):
                    b = i * 2 + s
                    wait(sp, moe_ps, at(moe_ps, TT, i, s, 2))
                    sp.dma_start(picks[:, s], pt_d[b]).then_inc(in_s[s].sem, 16)
                    wait(sp, summed, at(summed, TT, i, s, 2))
                    for dst, src in ((x_in, x_d), (attn, attn_d)):
                        sp.dma_start(dst[:, s], src[b].rearrange("(t p) d -> p t d", p=P)).then_inc(in_s[s].sem, 16)
                    src = inter_d[bass.ds(b * (T // NE), T // NE)].rearrange("(t c g) e d -> t (g e) c d", t=TT, c=C)
                    for t in range(TT):
                        wait(sp, moe_ps, at(moe_ps, t + 1, i, s, 1))
                        sp.dma_start(rows[:, t], src[t]).then_inc(rows_in[t].sem, 16)
                loop(sp, body)

            @block.gpsimd
            def _(pool):
                def body(i, s):
                    wait(pool, in_s[s], in_s[s].at(3, i))
                    pool.tensor_tensor(x_in[:, s], x_in[:, s], attn[:, s], ALU.add).then_inc(added.sem, 1)
                loop(pool, body)

            @block.scalar
            def _(act):
                def body(i, s):
                    wait(act, summed, at(summed, TT, i, s))
                    act.dma_start(out_d[i * 2 + s].rearrange("(t p) d -> p t d", p=P), out_sb[:, s])\
                       .then_inc(saved[s].sem, 16)
                loop(act, body)
                for s in range(2):
                    act.wait_ge(saved[s].sem, saved[s].at(1, B // 2 - 1))

            @block.vector
            def _(dve):
                def body(i, s):
                    wait(dve, saved[s], saved[s].at(0, i))
                    wait(dve, added, at(added, 1, i, s))
                    for t in range(TT):
                        wait(dve, moe_ps, at(moe_ps, t + 1, i, s))
                        dve.tensor_tensor(out_sb[:, s, t], banks[t][:, 0:D], x_in[:, s, t], ALU.add).then_inc(summed.sem, 1)
                loop(dve, body)

            @block.tensor
            def _(pe):
                def body(i, s):
                    wait(pe, in_s[s], in_s[s].at(3, i))
                    for t in range(TT):
                        wait(pe, rows_in[t], at(rows_in[t], 1, i, s))
                        wait(pe, summed, at(summed, t + 1, i, s, 1))
                        for g in range(C):
                            at32 = t * P + 32 * g
                            ins = pe.matmul(banks[t][32 * g:32 * g + 32, 0:D], picks[:, s, at32:at32 + 32], rows[:, t, g],
                                            start=True, stop=True, skip_group_check=True)
                        ins.then_inc(moe_ps.sem, 1)
                loop(pe, body)


_INS = ["L0_attn_x", "L0_attn_W_DKV", "L0_attn_W_UK", "L0_attn_W_UV", "L0_attn_W_UQ", "L0_attn_W_O",
        "L0_ffn_w1_w", "L0_ffn_w1_s", "L0_ffn_w2_w", "L0_ffn_w2_s", "L0_ffn_h1_w", "L0_ffn_h1_s",
        "L0_ffn_h2_w", "L0_ffn_h2_s", "L0_ffn_w3_w", "L0_ffn_w3_s", "L1_attn_Wqkv", "L1_attn_Wout",
        "L1_attn_Wpos", "L1_attn_coeffs", "L1_ffn_controller", "L1_ffn_f1", "L1_ffn_f2", "L1_ffn_bias"]
_TRANSPOSED = {"L0_ffn_w1_w", "L0_ffn_w2_w", "L0_ffn_h1_w", "L0_ffn_h2_w", "L0_ffn_w3_w", "L1_attn_Wqkv",
               "L1_attn_Wout", "L1_attn_Wpos", "L1_ffn_bias"}
_FLAT = {"L1_ffn_controller": (D, E), "L1_ffn_f1": (D, E * ESZ), "L1_ffn_f2": (E * ESZ, D), "L1_ffn_bias": (E, ESZ)}
_BY_TILE = {"L0_ffn_w1_s", "L0_ffn_w2_s", "L0_ffn_h1_s", "L0_ffn_h2_s"}


def program(nc, a, out, c):
    def scratch(name, shape, dt=F32):
        return nc.dram_tensor(name, shape, dt, kind=SCRATCH).ap()

    xh_d, xl_d = scratch("xh", [B, P, KD, T]), scratch("xl", [B, P, KD, T])
    attn_d = scratch("attn", [B, T, D])

    def place0(name, stage, ap):
        if name in "kv":
            return [(stage[r:r + LATENT, 0], ap) for r in (0, LATENT)]
        return [(stage[:, :, 0:ap.shape[1]], ap.rearrange("(k p) n -> p k n", p=P))]

    w0 = {"loads": [("q", a["L0_attn_W_UQ"], D), ("k", a["L0_attn_W_UK"], LATENT), ("v", a["L0_attn_W_UV"], LATENT),
                    ("c", a["L0_attn_W_DKV"], D)], "wo": a["L0_attn_W_O"], "place": place0}
    attention(nc, "l0", 0, a["L0_attn_x"], attn_d, xh_d, xl_d, None, w0, c)
    x1_d = scratch("x1", [B, T, D])
    lo_d = {m: scratch(f"lo_{m}", list(a[f"L0_ffn_{m}_w"].shape)) for m in ("w1", "w2", "h1", "h2", "w3")}
    ffn(nc, a["L0_attn_x"], attn_d, xh_d, xl_d, x1_d, {k[7:]: v for k, v in a.items() if k.startswith("L0_ffn_")}, c, lo_d)

    def place1(name, stage, ap):
        return [(stage[:, :, 0:D], ap.rearrange("(k p) n -> p k n", p=P))]

    ext_d = scratch("ext", [H, 2 * T])
    bias_table(nc, a["L1_attn_Wpos"], a["L1_attn_coeffs"], ext_d, c)
    yh_d, yl_d, yn_d = scratch("yh", [B, P, KD, T]), scratch("yl", [B, P, KD, T]), scratch("yn", [B, P, TT, D])
    attn1_d = scratch("attn1", [B, T, D])
    wqkv = a["L1_attn_Wqkv"]
    w1 = {"loads": [(name, wqkv[:, n * D:(n + 1) * D], D) for n, name in enumerate("qkv")],
          "wo": a["L1_attn_Wout"], "place": place1, "ext": ext_d}
    attention(nc, "l1", 1, x1_d, attn1_d, yh_d, yl_d, yn_d, w1, c)
    pt_d, inter_d = scratch("pt", [B, P, T]), scratch("inter", [GROUPS, E, D])
    with nc.sbuf_tensor("sel", [P, KD, E, GROUPS], F32) as sel:
        select(nc, sel, yh_d, yl_d, yn_d, pt_d, a["L1_ffn_controller"], c)
        experts(nc, sel, inter_d, a["L1_ffn_f1"], a["L1_ffn_f2"], a["L1_ffn_bias"], c)
    combine(nc, inter_d, pt_d, x1_d, attn1_d, out)


SCRATCH = "Internal"


def kernel(**inputs):
    import concourse.bacc as _bacc
    from concourse.bass_utils import run_bass_kernel_spmd as _run

    nc = _bacc.Bacc("TRN2", target_bir_lowering=False, num_devices=1)
    arrays, aps, cs = {}, {}, {}
    for name in _INS:
        x = np.asarray(inputs[name])
        if name in _FLAT:
            x = x.reshape(_FLAT[name])
        if name in _BY_TILE:
            x = x.reshape(-1, P).T
        arrays[f"in_{name}"] = np.ascontiguousarray(x.T if name in _TRANSPOSED else x)
    arrays.update(consts())
    for name, x in arrays.items():
        ap = nc.dram_tensor(name, x.shape, mybir.dt.from_np(x.dtype), kind="ExternalInput").ap()
        (cs if name.startswith("c_") else aps)[name.removeprefix("in_")] = ap
    out = nc.dram_tensor("out", (B, T, D), F32, kind="ExternalOutput").ap()
    program(nc, aps, out, cs)
    r = _run(nc, [arrays], core_ids=[0])
    return r.results[0]["out"]
```

```python
from contextlib import ExitStack

import numpy as np

import concourse.bass as bass
from concourse import mybir

F32 = mybir.dt.float32
F32R = mybir.dt.float32r
ALU = mybir.AluOpType
ACT = mybir.ActivationFunctionType
AX_X = mybir.AxisListType.X

P = 128
B, T, D = 8, 512, 256
KD = D // P
TT = T // P
H, HD = 16, 16
PAIRS = H // 2
QUADS = H // 4
HROWS = P // 2
LATENT = 64
HID = 1024
KH = HID // P
NE, ES, ESZ = 16, 4, 64
E = NE * ES
GROUPS = B * T // NE
RES, TAPS = 128, 101
NEG = -1.0e30
MIN_N = 256
PARTS = ((0, 1), (1, 0), (0, 0))
EPS = 1.0e-5
UW = 2 * T - P
UOFF = T - P


class Tally:

    def __init__(self, sem, per=0, grant=0, unit=1):
        self.sem, self.per, self.grant, self.unit = sem, per * unit, grant * unit, unit

    def at(self, k, i=0):
        return i * self.per + (self.grant + k * self.unit)


def consts():
    row = np.arange(P) % HROWS
    cols = np.zeros((P, 4), np.float32)
    cols[(row // HD) == 1, 0] = -1.0
    cols[(row // HD) == 2, 1] = -1.0
    cols[row == 3 * HD, 1] = 1.0
    cols[row == 3 * HD, 2] = -1.0
    cols[LATENT:, 3] = -1.0
    mask = np.zeros((P, T), np.float32)
    mask[:, T - P:] = np.where(np.arange(P)[None, :] <= np.arange(P)[:, None], 0.0, NEG)
    ramp = np.linspace(0.0, 1.0, RES).astype(np.float32)
    dist = np.abs(np.arange(2 * T) - (T - 1)).astype(np.float32) / np.float32(T - 1)
    idx = np.clip(np.round(dist * np.float32(RES - 1)).astype(np.int32), 0, RES - 1)
    n = idx[None, :] - np.arange(TAPS)[:, None]
    fir = np.where(n >= 0, ramp[np.clip(n, 0, RES - 1)], 0.0).astype(np.float32)
    step = np.arange(NE, dtype=np.float32) / np.float32(NE - 1)
    tie = np.tile(np.float32(1e-6) * step, (P, T // NE)).astype(np.float32)
    group = (np.arange(P)[:, None] // NE == np.arange(P // NE)[None, :]).astype(np.float32)
    odd = (np.arange(T)[None, :] // NE % 2 == np.arange(P)[:, None] // E).astype(np.float32)
    return {"c_parity": odd, "c_flip": np.ascontiguousarray(np.eye(P, dtype=np.float32)[::-1]), "c_ident": np.eye(P, dtype=np.float32), "c_cols": cols, "c_mask": mask, "c_fir": fir,
            "c_tie": tie, "c_group": group, "c_pow": np.full((P, TT), -0.5, np.float32)}


def clear(nc, tallies):
    with nc.Block() as block:
        @block.sync
        def _(sp):
            for tally in tallies:
                sp.sem_clear(tally.sem)


def attention(nc, tag, layer, x_d, out_d, xh_d, xl_d, xn_d, w, c):
    causal = layer == 0
    with ExitStack() as ctx:
        def sb(name, shape, dt=F32):
            return ctx.enter_context(nc.sbuf_tensor(f"{tag}_{name}", shape, dt))

        tallies = []

        def sem(name, per=0, grant=0, unit=1):
            tallies.append(Tally(ctx.enter_context(nc.semaphore(f"{tag}_{name}")), per, grant, unit))
            return tallies[-1]

        ident, cols = sb("ident", [P, P]), sb("cols", [P, 4])
        power = sb("power", [P, TT])
        q_low, k_low, k_one, c_low = (cols[:, j:j + 1] for j in range(4))
        wq = sb("wq", [P, 2, KD, PAIRS, P], F32R)
        KK = 1 if causal else KD
        wk = sb("wk", [P, 2, KK, PAIRS, P], F32R)
        wv = sb("wv", [P, 2, KK, D], F32R)
        wo = sb("wo", [P, KD, D])
        if causal:
            wc = sb("wc", [P, 2, KD, P], F32R)
            mask = sb("mask", [P, T])
        else:
            bias = sb("bias", [P, H, UW])
        x_in, xn = sb("x_in", [P, TT, D]), sb("xn", [P, TT, D])
        stats, moments = sb("stats", [P, TT, 6]), sb("moments", [P, TT, 2])
        var_eps, rstd = sb("var_eps", [P, TT]), sb("rstd", [P, TT])
        xh, xl = sb("xh", [P, KD, T], F32R), sb("xl", [P, KD, T], F32R)
        cs = sb("cs", [P, T], F32R) if causal else None
        top = sb("top", [P, 2, T], F32R)
        qs, ks = sb("qs", [P, QUADS, 2, T], F32R), sb("ks", [P, QUADS, 2, 2, T], F32R)
        vals_sb = sb("vals", [P, TT * H * (HD + 1) + 32])
        vals = vals_sb[:, 0:TT * H * (HD + 1)].rearrange("p (t h d) -> p t h d", t=TT, h=H)
        peak = sb("peak", [P, TT, 2, P])
        prob = sb("prob", [P, 4, 2, T])
        o_sb = sb("o_sb", [P, T])
        inv = sb("inv", [P, QUADS, TT, 4])
        mix, mixt = sb("mix", [P, TT, D]), sb("mixt", [P, KD, T])
        out_sb = sb("out_sb", [P, TT, D])

        banks = [ctx.enter_context(nc.psum_tensor(f"{tag}_ps{j}", [P, T], F32)) for j in range(8)]
        a_bank, b_bank, m_bank, o_bank, misc = banks[0:2], banks[2:4], banks[4], banks[5], banks[6:8]

        consts_in = sem("consts_in", unit=16)
        w_in = sem("w_in", unit=16)
        w_hi, w_ready, zeroed = sem("w_hi"), sem("w_ready"), sem("zeroed")
        x_loaded = sem("x_loaded", 1, unit=16)
        x_saved = sem("x_saved", 2 if causal else 3, unit=16)
        out_saved = sem("out_saved", 1, grant=1, unit=16)
        stats_done, moments_done = sem("stats_done", TT), sem("moments_done", TT)
        eps_done, rstd_ready, xn_ready = sem("eps_done", 1), sem("rstd_ready", 1), sem("xn_ready", TT)
        xt_ps, xh_ready, xl_ready = sem("xt_ps", KD), sem("xh_ready", KD), sem("xl_ready", KD)
        c_ps, c_top, c_ready = sem("c_ps", 1), sem("c_top", 1), sem("c_ready", 1)
        v_ps, v_ready = sem("v_ps", 2), sem("v_ready", 2)
        s_ps, s_top, s_ready = (sem(n, 2 * PAIRS) for n in ("s_ps", "s_top", "s_ready"))
        a_ps, a_max = sem("a_ps", 4 * H), sem("a_max", 4 * H)
        m_ps, qm_ready = sem("m_ps", PAIRS), sem("qm_ready", PAIRS)
        b_ps, p_exp, p_done = sem("b_ps", 4 * H), sem("p_exp", 4 * H), sem("p_done", 4 * H)
        pv_ps, o_copied, ot_ps = sem("pv_ps", QUADS), sem("o_copied", QUADS), sem("ot_ps", QUADS)
        inv_ready, mix_ready = sem("inv_ready", QUADS), sem("mix_ready", QUADS)
        mt_ps, mixt_ready = sem("mt_ps", KD), sem("mixt_ready", KD)
        out_ps, out_ready = sem("out_ps", 2), sem("out_ready", 2)

        flip = o_sb[:, 0:P]
        rising = [prob[:, a].rearrange("p j t -> p (j t)")[:, 0:UW] for a in range(4)]
        rising_in = [sem(f"rising_in{a}", unit=16) for a in range(4)] if not causal else None
        bias_ps, bias_ready = sem("bias_ps"), sem("bias_ready")

        POOLED = (0, 1, 3, 5, 7)
        p_add = [sem("p_add0", H // 2 * (8 - len(POOLED))), sem("p_add1", H // 2 * len(POOLED))]
        p_copied = sem("p_copied", H // 2 * len(POOLED))
        held_dve, held_pool = sem("held_dve"), sem("held_pool")

        w_low = sem("w_low")
        with nc.sbuf_tensor(f"{tag}_stage", [P, KD, D], F32) as stage_w, \
             nc.sbuf_tensor(f"{tag}_hi", [P, KD, D], F32R) as hi_w, nc.Block() as block:
            def parts(name):
                kk, wide = (1 if (causal and name in "kv") else KD), (LATENT if name == "c" else D)
                return stage_w[:, 0:kk, 0:wide], hi_w[:, 0:kk, 0:wide]

            def placed(name, part, src):
                if name in "qk":
                    scale = HD ** -0.5 if name == "k" else 1.0
                    for k in range(src.shape[1]):
                        dst = (wq if name == "q" else wk)[:, part, k].rearrange("p g (a s d) -> p (g a) s d", a=2, s=4)
                        for slot in range(3):
                            yield dst[:, :, slot, :], src[:, k].rearrange("p (h d) -> p h d", d=HD), scale
                elif name == "v":
                    yield wv[:, part], src, 1.0
                else:
                    for twice in range(2):
                        yield wc[:, part, :, twice * LATENT:(twice + 1) * LATENT], src, 1.0

            @block.sync
            def _(sp):
                sp.dma_start(ident[:], c["c_ident"]).then_inc(consts_in.sem, 16)
                sp.dma_start(cols[:], c["c_cols"]).then_inc(consts_in.sem, 16)
                sp.dma_start(power[:], c["c_pow"]).then_inc(consts_in.sem, 16)
                sp.dma_start(wo[:], w["wo"].rearrange("(k p) n -> p k n", p=P)).then_inc(consts_in.sem, 16)
                if causal:
                    sp.dma_start(mask[:], c["c_mask"]).then_inc(consts_in.sem, 16)
                else:
                    sp.dma_start(flip, c["c_flip"]).then_inc(consts_in.sem, 16)
                for n, (name, ap) in enumerate(w["loads"]):
                    if n:
                        sp.wait_ge(w_ready.sem, n)
                        sp.wait_ge(w_low.sem, n)
                    for dst, src in w["place"](name, stage_w, ap):
                        sp.dma_start(dst, src).then_inc(w_in.sem, 16)
                sp.wait_ge(consts_in.sem, 16 * 5)
            @block.scalar
            def _(act):
                def bias_rows(first, last):
                    for n in range(first, last):
                        h, half = n // 2, n % 2
                        act.wait_ge(bias_ps.sem, n + 1)
                        act.activation(bias[:, h, half * (UW // 2):(half + 1) * (UW // 2)], banks[n % 8][:, 0:UW // 2],
                                       ACT.Copy).then_inc(bias_ready.sem, 1)

                for n, (name, ap) in enumerate(w["loads"]):
                    raw, hi = parts(name)
                    if not causal:
                        bias_rows(8 * n, 8 * n + 8)
                    act.wait_ge(w_hi.sem, n * 2 + 2)
                    for dst, src, scale in placed(name, 1, raw):
                        last = act.activation(dst, src, ACT.Copy, scale=scale)
                    last.then_inc(w_low.sem, 1)
                if not causal:
                    bias_rows(8 * len(w["loads"]), 2 * H)

            if not causal:
                @block.tensor
                def _(pe):
                    pe.wait_ge(consts_in.sem, 16 * 5)
                    for n in range(2 * H):
                        h, half = n // 2, n % 2
                        pe.wait_ge(rising_in[h % 4].sem, 16 * (h // 4 + 1))
                        if n >= 8:
                            pe.wait_ge(bias_ready.sem, n - 7)
                        pe.matmul(banks[n % 8][:, 0:UW // 2], flip, rising[h % 4][:, half * (UW // 2):(half + 1) * (UW // 2)],
                                  start=True, stop=True).then_inc(bias_ps.sem, 1)

            @block.vector
            def _(dve):
                for dst in (wq, wk):
                    dve.memset(dst[:].rearrange("p q k g (a s d) -> p (q k g a) s d", a=2, s=4)[:, :, 3].bitcast(F32), 0.0)\
                       .then_inc(zeroed.sem, 1)
                dve.memset(vals_sb[:], 0.0).then_inc(zeroed.sem, 1)
                dve.wait_ge(zeroed.sem, 3)
                dve.memset(vals[:, :, :, HD:HD + 1], 1.0).then_inc(zeroed.sem, 1)
                loaded = 0
                for n, (name, ap) in enumerate(w["loads"]):
                    loaded += 16 * len(w["place"](name, stage_w, ap))
                    raw, hi = parts(name)
                    dve.wait_ge(w_in.sem, loaded)
                    if n:
                        dve.wait_ge(w_ready.sem, n)
                    dve.tensor_copy(hi, raw).then_inc(w_hi.sem, 1)
                    dve.wait_ge(w_hi.sem, n * 2 + 1)
                    dve.tensor_tensor(raw, raw, hi.bitcast(F32), ALU.subtract).then_inc(w_hi.sem, 1)
                    dve.wait_ge(w_hi.sem, n * 2 + 2)
                    for dst, src, scale in placed(name, 0, hi.bitcast(F32)):
                        last = dve.tensor_scalar(dst, src, scale, None, ALU.mult)
                    last.then_inc(w_ready.sem, 1)

            @block.gpsimd
            def _(pool):
                def rise(first, last):
                    for h in range(first, last):
                        if h >= 4:
                            pool.wait_ge(bias_ps.sem, 2 * (h - 3))
                        src = bass.AP(w["ext"].tensor, w["ext"].offset + h * 2 * T, [[1, P], [1, UW]])
                        pool.dma_start(rising[h % 4], src).then_inc(rising_in[h % 4].sem, 16)

                if not causal:
                    rise(0, 4)
                pool.memset(peak[:], 0.0)
                pool.memset(ks[:].bitcast(F32), 0.0)
                if not causal:
                    rise(4, H)

        SLOTS = 4 * TT + 2
        STEADY = []
        LAG = 1 if causal else 2
        VALUES, LAST = ((8, 13, 17), 3) if causal else ((10, 13, 17), 5)
        STACKS = (3, 7, 11, 14) if causal else (3, 7, 11, 15)
        for s in range(QUADS):
            before, before2 = ((0, s - 1) if s else (-1, QUADS - 1)), ((0, s - 2) if s > 1 else (-1, s + 2))
            after = (0, s + 1) if s + 1 < QUADS else (1, 0)
            for slot in range(SLOTS):
                if slot < 16:
                    STEADY.append(("score", 0, 16 * s + slot))
                if slot == 1:
                    STEADY.append(("maxima", before[0], 2 * before[1] + 1))
                if slot == 11:
                    STEADY.append(("maxima", 0, 2 * s))
                if slot == LAST:
                    STEADY.append(("value", before2[0], TT * before2[1] + TT - 1))
                if slot in VALUES:
                    STEADY.append(("value", before[0], TT * before[1] + VALUES.index(slot)))
                if slot >= 2:
                    STEADY.append(("prob", before[0], 16 * before[1] + slot - 2))
                n = slot - 2 - LAG
                if n >= 0:
                    STEADY.append(("prob_exp", before[0], 16 * before[1] + n))
                elif n + SLOTS < 16:
                    STEADY.append(("prob_exp", before2[0], 16 * before2[1] + n + SLOTS))
                for kind, at in (("stack", STACKS), ("stack_top", [n + 1 for n in STACKS]),
                                 ("stack_low", [n + 2 for n in STACKS])):
                    if slot in at:
                        STEADY.append((kind, after[0], 4 * after[1] + at.index(slot)))
                if slot == 4:
                    STEADY.append(("heads_copy", before2[0], before2[1]))
                if slot == 6:
                    STEADY.append(("heads_turn", before2[0], before2[1]))
                if slot == 8:
                    STEADY.append(("heads_norm", before2[0], before2[1]))
                STEADY += {(1, 5): [("v", 0, 0), ("v", 0, 1)],
                           (1, 10): [("mix_turn", -1, 0), ("mix_turn", -1, 1), ("ln_stats", 1, 0)],
                           (1, 13): [("out", -1, 0), ("out", -1, 1)],
                           (1, 15): [("store", -1, 0)],
                           (2, 6): [("ln", 1, 0)],
                           (2, 16): [("x_turn", 1, 0), ("x_turn", 1, 1)],
                           (2, 17): [("x_high", 1, 0), ("x_high", 1, 1)],
                           (3, 0): [("x_low", 1, 0), ("x_low", 1, 1)],
                           (3, 1): [("latent", 1, 0)] * causal,
                           (3, 2): [("latent_top", 1, 0)] * causal,
                           (3, 3): [("latent_low", 1, 0)] * causal}.get((s, slot), [])

        LAST_READ = {"stack": s_ready, "heads_turn": mix_ready, "v": v_ready, "mix_turn": mixt_ready,
                     "out": out_ready, "x_turn": xl_ready}
        USES = [e for e in STEADY if e[0] in LAST_READ]
        assert len(USES) % 2 == 0

        def bank(kind, n):
            return misc[[(u[0], u[2]) for u in USES].index((kind, n)) % 2]

        def there(b):
            return not isinstance(b, int) or 0 <= b < B

        def turns(eng, emit):
            def turn(i):
                for kind, off, n in STEADY:
                    if there(i + off):
                        emit(kind, i + off, n, i)
            turn(-1)
            turn(0)
            with eng.Fori(1, B - 1) as i:
                turn(i)
            turn(B - 1)
            turn(B)

        def wait(eng, tally, k, b):
            value = tally.at(k, b)
            if not isinstance(value, int) or value > 0:
                eng.wait_ge(tally.sem, value)

        def hold(eng, held, tally, k, b):
            wait(eng, tally, k, b)
            if not isinstance(b, int):
                eng.sem_inc(held.sem, 1)

        def keys_of(n):
            j, a = n % 16 // 4, n % 4
            wide = max(T - j * P, MIN_N) if causal else T
            return n // 16, j, a, wide, T - wide

        def pooled(n):
            return n % 8 in POOLED

        def nth(n):
            return sum(pooled(m) == pooled(n) for m in range(n + 1))

        def add_bias(eng, b, n, src):
            g, j, a, wide, q0 = keys_of(n)
            eng.tensor_tensor(prob[:, a, j % 2], src, bias[:, 4 * g + a, UOFF - j * P:UOFF - j * P + T],
                              ALU.add).then_inc(p_add[pooled(n)].sem, 1)

        with nc.Block() as block:
            @block.sync
            def _(sp):
                saves = 2 if causal else 3

                def load(b):
                    sp.dma_start(x_in[:], x_d[b].rearrange("(t p) d -> p t d", p=P)).then_inc(x_loaded.sem, 16)

                def save(b):
                    wait(sp, xh_ready, KD, b)
                    sp.dma_start(xh_d[b], xh[:].bitcast(F32)).then_inc(x_saved.sem, 16)
                    wait(sp, xl_ready, KD, b)
                    sp.dma_start(xl_d[b], xl[:].bitcast(F32)).then_inc(x_saved.sem, 16)
                    if not causal:
                        sp.dma_start(xn_d[b], xn[:]).then_inc(x_saved.sem, 16)
                    wait(sp, x_saved, saves, b)

                load(0)
                with sp.Fori(0, B - 1) as i:
                    save(i)
                    load(i + 1)
                save(B - 1)

            @block.gpsimd
            def _(pool):
                def emit(kind, b, n, i):
                    if kind == "ln_stats":
                        wait(pool, eps_done, 1, b)
                        nc.gpsimd.tensor_tensor(rstd[:], var_eps[:], power[:], ALU.pow).then_inc(rstd_ready.sem, 1)
                    if kind == "prob" and causal:
                        g, j, a, wide, q0 = keys_of(n)
                        hold(pool, held_pool, p_exp, n + 1, b)
                        blk = prob[:, a, j % 2, j * P:(j + 1) * P]
                        nc.gpsimd.affine_select(out=blk, in_=blk, compare_op=ALU.is_ge, fill=0.0, base=0,
                                                pattern=[[1, P]], channel_multiplier=-1).then_inc(p_done.sem, 1)
                    if kind == "prob" and not causal and pooled(n):
                        g, j, a, wide, q0 = keys_of(n)
                        wait(pool, p_copied, nth(n), b)
                        add_bias(pool, b, n, prob[:, a, j % 2])
                turns(pool, emit)

            @block.scalar
            def _(act):
                act.sem_inc(out_saved.sem, 16)

                def emit(kind, b, n, i):
                    if kind == "x_high":
                        wait(act, xt_ps, n + 1, b)
                        act.copy(xh[:, n], bank("x_turn", n)[:]).then_inc(xh_ready.sem, 1)
                    if kind == "latent_top":
                        wait(act, c_ps, 1, b)
                        act.copy(top[:, 0], m_bank[:]).then_inc(c_top.sem, 1)
                    if kind == "v":
                        wait(act, v_ps, n + 1, b)
                        act.copy(vals[:, 2 * n:2 * n + 2, :, 0:HD],
                                 bank("v", n)[:].rearrange("p (t h d) -> p t h d", t=2, d=HD)).then_inc(v_ready.sem, 1)
                    if kind == "stack_top":
                        wait(act, s_ps, n + 1, b)
                        if causal and n == 0:
                            wait(act, c_ready, 1, b)
                        wait(act, s_ready, n - 1, b)
                        src = bank("stack", n)[:]
                        if n % 2 == 0:
                            act.activation(top[:, 0], src, ACT.Copy).then_inc(s_top.sem, 1)
                        else:
                            act.activation(top[:, 1], src, ACT.Identity, bias=k_one).then_inc(s_top.sem, 1)
                    if kind == "prob_exp" and causal:
                        g, j, a, wide, q0 = keys_of(n)
                        wait(act, b_ps, n + 1, b)
                        act.activation(prob[:, a, j % 2, j * P:T], b_bank[n % 2][:, j * P - q0:wide],
                                       ACT.Exp).then_inc(p_exp.sem, 1)
                    if kind == "prob" and not causal and pooled(n):
                        g, j, a, wide, q0 = keys_of(n)
                        wait(act, b_ps, n + 1, b)
                        act.activation(prob[:, a, j % 2], b_bank[n % 2][:], ACT.Copy).then_inc(p_copied.sem, 1)
                    if kind == "prob_exp" and not causal:
                        g, j, a, wide, q0 = keys_of(n)
                        wait(act, p_add[pooled(n)], nth(n), b)
                        act.activation(prob[:, a, j % 2], prob[:, a, j % 2], ACT.Exp).then_inc(p_done.sem, 1)
                    if kind == "heads_copy":
                        wait(act, pv_ps, n + 1, b)
                        act.copy(o_sb[:], o_bank[:]).then_inc(o_copied.sem, 1)
                    if kind == "mix_turn":
                        wait(act, mt_ps, n + 1, b)
                        act.copy(mixt[:, n], bank(kind, n)[:]).then_inc(mixt_ready.sem, 1)
                    if kind == "out":
                        if n == 0:
                            wait(act, out_saved, 1, b - 1)
                        wait(act, out_ps, n + 1, b)
                        act.copy(out_sb[:, 2 * n:2 * n + 2],
                                 bank(kind, n)[:].rearrange("p (t d) -> p t d", t=2)).then_inc(out_ready.sem, 1)
                    if kind == "store":
                        wait(act, out_ready, 2, b)
                        act.dma_start(out_d[b].rearrange("(t p) d -> p t d", p=P), out_sb[:]).then_inc(out_saved.sem, 16)
                turns(act, emit)
                act.wait_ge(out_saved.sem, out_saved.at(1, B - 1))

            @block.vector
            def _(dve):
                def emit(kind, b, n, i):
                    if kind == "ln_stats":
                        wait(dve, x_loaded, 1, b)
                        for t in range(TT):
                            dve.bn_stats(stats[:, t], x_in[:, t]).then_inc(stats_done.sem, 1)
                        for t in range(TT):
                            hold(dve, held_dve, stats_done, t + 1, b)
                            dve.bn_aggr(moments[:, t], stats[:, t]).then_inc(moments_done.sem, 1)
                        wait(dve, moments_done, TT, b)
                        dve.tensor_scalar(var_eps[:], moments[:, :, 1], EPS, None, ALU.add).then_inc(eps_done.sem, 1)
                    if kind == "ln":
                        wait(dve, rstd_ready, 1, b)
                        for t in range(TT):
                            dve.tensor_scalar(xn[:, t], x_in[:, t], moments[:, t, 0:1], rstd[:, t:t + 1],
                                              ALU.subtract, ALU.mult).then_inc(xn_ready.sem, 1)
                    if kind == "x_low":
                        wait(dve, xh_ready, n + 1, b)
                        dve.tensor_tensor(xl[:, n], bank("x_turn", n)[:], xh[:, n].bitcast(F32),
                                          ALU.subtract).then_inc(xl_ready.sem, 1)
                    if kind == "latent_low":
                        wait(dve, c_top, 1, b)
                        dve.scalar_tensor_tensor(cs[:], top[:, 0].bitcast(F32), c_low, m_bank[:],
                                                 ALU.mult, ALU.add).then_inc(c_ready.sem, 1)
                    if kind == "stack_low":
                        wait(dve, s_top, n + 1, b)
                        g, pr, src = n // 4, n // 2 % 2, bank("stack", n)
                        if n % 2 == 0:
                            dve.scalar_tensor_tensor(qs[:, g, pr], top[:, 0].bitcast(F32), q_low, src[:],
                                                     ALU.mult, ALU.add).then_inc(s_ready.sem, 1)
                        else:
                            for a in range(2):
                                r = slice(a * HROWS, (a + 1) * HROWS)
                                ins = dve.scalar_tensor_tensor(ks[r, g, pr, a], top[r, 1].bitcast(F32), k_low[r],
                                                               src[r, :], ALU.mult, ALU.add)
                            ins.then_inc(s_ready.sem, 1)
                    if kind == "maxima":
                        g, pr = n // 2, n % 2
                        wait(dve, m_ps, n + 1, b)
                        dve.tensor_tensor(qs[:, g, pr], m_bank[:], qs[:, g, pr].bitcast(F32), ALU.add)\
                           .then_inc(qm_ready.sem, 1)
                    if kind == "score":
                        pr, t, a = n // 8 % 2, n // 2 % 4, n % 2
                        wide = (t + 1) * P if causal else T
                        add = mask[:, T - wide:T] if causal else \
                            bias[:, 4 * (n // 16) + 2 * pr + a, UOFF - t * P:UOFF - t * P + T]
                        src = a_bank[n % 2][:, 0:wide]
                        col = a * HROWS + 3 * HD
                        hold(dve, held_dve, a_ps, n + 1, b)
                        dve.tensor_tensor_reduce(src, src, add, 1.0, 3 * NEG, ALU.add, ALU.max,
                                                 peak[:, t, pr, col:col + 1]).then_inc(a_max.sem, 1)
                    if kind == "prob" and not causal and not pooled(n):
                        wait(dve, b_ps, n + 1, b)
                        add_bias(dve, b, n, b_bank[n % 2][:])
                    if kind == "heads_norm":
                        wait(dve, ot_ps, n + 1, b)
                        src = bank("heads_turn", n)[:].rearrange("p (t a d) -> p t a d", t=TT, a=4)
                        dve.reciprocal(inv[:, n], src[:, :, :, HD]).then_inc(inv_ready.sem, 1)
                        wait(dve, inv_ready, n + 1, b)
                        dst = mix[:].rearrange("p t (g a d) -> p t g a d", g=QUADS, a=4)[:, :, n]
                        dve.tensor_tensor(dst, src[:, :, :, 0:HD], inv[:, n].unsqueeze(3).to_broadcast([P, TT, 4, HD]),
                                          ALU.mult).then_inc(mix_ready.sem, 1)
                turns(dve, emit)

            @block.tensor
            def _(pe):
                def claim(kind, n, i):
                    names = [(u[0], u[2]) for u in USES]
                    at = names.index((kind, n))
                    for m in range(at - 2, at - len(USES) - 1, -2):
                        before, off, k = USES[m]
                        bb = i + off - (1 if m < 0 else 0)
                        if there(bb):
                            wait(pe, LAST_READ[before], k + 1, bb)
                            break
                    return misc[at % 2]

                def product(out, pairs):
                    for m, (left, right) in enumerate(pairs):
                        ins = pe.matmul(out, left, right, start=(m == 0), stop=(m == len(pairs) - 1))
                    return ins

                def emit(kind, b, n, i):
                    if kind == "x_turn":
                        out = claim(kind, n, i)
                        wait(pe, xn_ready, TT, b)
                        for t in range(TT):
                            ins = pe.transpose(out[:, t * P:(t + 1) * P], xn[:, t, n * P:(n + 1) * P], ident[:])
                        ins.then_inc(xt_ps.sem, 1)
                    if kind == "latent":
                        wait(pe, qm_ready, PAIRS - 2, b - 1)
                        wait(pe, xl_ready, KD, b)
                        product(m_bank[:], [(wc[:, p, k], (xl if q else xh)[:, k]) for k in range(KD)
                                            for p, q in PARTS]).then_inc(c_ps.sem, 1)
                    if kind == "v":
                        out = claim(kind, n, i)
                        wait(pe, c_ready if causal else xl_ready, 1 if causal else KD, b)
                        for t in range(2 * n, 2 * n + 2):
                            o = out[:, (t % 2) * D:(t % 2 + 1) * D]
                            cut = slice(t * P, (t + 1) * P)
                            if causal:
                                ins = product(o, [(cs[:, cut], wv[:, p, 0]) for p in (1, 0)])
                            else:
                                ins = product(o, [((xl if q else xh)[:, k, cut], wv[:, p, k]) for k in range(KD)
                                                  for p, q in PARTS])
                        ins.then_inc(v_ps.sem, 1)
                    if kind == "stack":
                        out = claim(kind, n, i)
                        if n % 2 and causal:
                            wait(pe, c_ready, 1, b)
                            pairs = [(wk[:, p, 0, n // 2], cs[:]) for p in (1, 0)]
                        else:
                            wait(pe, xl_ready, KD, b)
                            pairs = [((wk if n % 2 else wq)[:, p, k, n // 2], (xl if q else xh)[:, k])
                                     for k in range(KD) for p, q in PARTS]
                        product(out[:], pairs).then_inc(s_ps.sem, 1)
                    if kind == "score":
                        g, pr, t, a = n // 16, n // 8 % 2, n // 2 % 4, n % 2
                        if n % 16 in (0, 8):
                            wait(pe, s_ready, 4 * g + 2 * pr + 2, b)
                        wait(pe, a_max, n - 1, b)
                        wide = max((t + 1) * P, MIN_N) if causal else T
                        pe.matmul(a_bank[n % 2][:, 0:wide], qs[:, g, pr, t * P:(t + 1) * P],
                                  ks[:, g, pr, a, 0:wide], start=True, stop=True).then_inc(a_ps.sem, 1)
                    if kind == "maxima":
                        g, pr = n // 2, n % 2
                        wait(pe, a_max, 16 * g + 8 * pr + 8, b)
                        wait(pe, qm_ready, n, b)
                        if causal and n == 0:
                            wait(pe, c_ready, 1, b)
                        for t in range(TT):
                            ins = pe.transpose(m_bank[:, t * P:(t + 1) * P], peak[:, t, pr], ident[:])
                        ins.then_inc(m_ps.sem, 1)
                    if kind == "prob":
                        g, j, a, wide, q0 = keys_of(n)
                        if n % 16 == 0:
                            wait(pe, qm_ready, 2 * g + 1, b)
                        if n % 16 == 2:
                            wait(pe, qm_ready, 2 * g + 2, b)
                        if causal:
                            wait(pe, p_exp, n - 1, b)
                        elif n >= 2:
                            wait(pe, p_copied if pooled(n - 2) else p_add[0], nth(n - 2), b)
                        else:
                            last = 4 * H - 2 + n
                            wait(pe, p_copied if pooled(last) else p_add[0], nth(last), b - 1)
                        pe.matmul(b_bank[n % 2][:, 0:wide], ks[:, g, a // 2, a % 2, j * P:(j + 1) * P],
                                  qs[:, g, a // 2, q0:T], start=True, stop=True).then_inc(b_ps.sem, 1)
                    if kind == "value":
                        g, j = n // TT, n % TT
                        if j == 0:
                            wait(pe, o_copied, g, b)
                        if n == 0:
                            wait(pe, v_ready, 2, b)
                        wait(pe, p_done, 16 * g + 4 * j + 4, b)
                        q0 = j * P if causal else 0
                        for a in range(4):
                            v0 = (j * H + 4 * g + a) * (HD + 1)
                            ins = pe.matmul(o_bank[32 * a:32 * a + 32, q0:T], vals_sb[:, v0:v0 + 32],
                                            prob[:, a, j % 2, q0:T], start=(j == 0), stop=(j == TT - 1),
                                            skip_group_check=True)
                        if j == TT - 1:
                            ins.then_inc(pv_ps.sem, 1)
                    if kind == "heads_turn":
                        out = claim(kind, n, i)
                        wait(pe, o_copied, n + 1, b)
                        for t in range(TT):
                            ins = pe.transpose(out[:, t * P:(t + 1) * P], o_sb[:, t * P:(t + 1) * P], ident[:])
                        ins.then_inc(ot_ps.sem, 1)
                    if kind == "mix_turn":
                        out = claim(kind, n, i)
                        wait(pe, mix_ready, QUADS, b)
                        for t in range(TT):
                            ins = pe.transpose(out[:, t * P:(t + 1) * P], mix[:, t, n * P:(n + 1) * P], ident[:])
                        ins.then_inc(mt_ps.sem, 1)
                    if kind == "out":
                        out = claim(kind, n, i)
                        wait(pe, mixt_ready, KD, b)
                        for t in range(2 * n, 2 * n + 2):
                            ins = product(out[:, (t % 2) * D:(t % 2 + 1) * D],
                                          [(mixt[:, k, t * P:(t + 1) * P], wo[:, k]) for k in range(KD)])
                        ins.then_inc(out_ps.sem, 1)
                turns(pe, emit)
        clear(nc, tallies)



class BiasTable:

    def __init__(self, nc, ctx, wpos, coeffs, ext_d, c, banks):
        def sb(name, shape):
            return ctx.enter_context(nc.sbuf_tensor(f"t_{name}", shape, F32))

        def sem(name):
            return ctx.enter_context(nc.semaphore(f"t_{name}"))

        self.sources, self.ext_d, self.banks = (wpos, coeffs, c["c_fir"]), ext_d, banks
        self.wpos, self.coeffs, self.fir = sb("wpos", list(wpos.shape)), sb("coeffs", list(coeffs.shape)), sb("fir", [TAPS, 2 * T])
        self.cw, self.ext = sb("cw", [TAPS, H]), sb("ext", [H, 2, T])
        self.loaded, self.cw_ps, self.cw_ready, self.ext_ps, self.ext_ready, self.saved = \
            (sem(n) for n in ("loaded", "cw_ps", "cw_ready", "ext_ps", "ext_ready", "saved"))

    def move(self, eng):
        for dst, src in zip((self.wpos, self.coeffs, self.fir), self.sources):
            eng.dma_start(dst[:], src).then_inc(self.loaded, 16)
        eng.wait_ge(self.ext_ready, 2)
        eng.dma_start(self.ext_d, self.ext[:].rearrange("h a t -> h (a t)")).then_inc(self.saved, 16)
        eng.wait_ge(self.saved, 16)

    def products(self, pe):
        pe.wait_ge(self.loaded, 16 * 3)
        pe.matmul(self.banks[0][0:TAPS, 0:H], self.coeffs[:], self.wpos[:], start=True, stop=True).then_inc(self.cw_ps, 1)
        pe.wait_ge(self.cw_ready, 1)
        for n in range(2):
            pe.matmul(self.banks[1 + n][0:H, :], self.cw[:], self.fir[:, n * T:(n + 1) * T], start=True, stop=True)\
              .then_inc(self.ext_ps, 1)

    def copies(self, act):
        act.wait_ge(self.cw_ps, 1)
        act.activation(self.cw[:], self.banks[0][0:TAPS, 0:H], ACT.Copy).then_inc(self.cw_ready, 1)
        for n in range(2):
            act.wait_ge(self.ext_ps, n + 1)
            act.activation(self.ext[:, n], self.banks[1 + n][0:H, :], ACT.Copy).then_inc(self.ext_ready, 1)


def ffn(nc, x_d, attn_d, xh_d, xl_d, out_d, w, c, lo_d, bias):
    with ExitStack() as ctx:
        def sb(name, shape, dt=F32):
            return ctx.enter_context(nc.sbuf_tensor(f"f_{name}", shape, dt))

        tallies = []

        def sem(name, per=0, grant=0, unit=1):
            tallies.append(Tally(ctx.enter_context(nc.semaphore(f"f_{name}")), per, grant, unit))
            return tallies[-1]

        names = ("w1", "w2", "h1", "h2", "w3")
        wide = {"w1": HID, "w2": HID, "h1": HID, "h2": HID, "w3": D}
        deep = {"w1": KD, "w2": KD, "h1": KH, "h2": KH, "w3": KH}
        hi = {m: sb(f"hi_{m}", [P, deep[m], wide[m]], F32R) for m in names}
        gate_s, both_s, h1_s, h2_s = (sb(n, [P, KH]) for n in ("gate_s", "both_s", "h1_s", "h2_s"))
        out_s = sb("out_s", [P, D])
        ident = sb("ident", [P, P])
        flag = sb("flag", [1, 1], mybir.dt.int32)
        low = sb("low", [P, 2, KH, P], F32R)
        psum = [ctx.enter_context(nc.psum_tensor(f"f_ps{j}", [P, T], F32)) for j in range(8)]

        CH, RING = 1024, 4
        chunks = [(m, k) for m in names for k in range(deep[m])]
        loaded = [sem(f"loaded{j}", unit=16) for j in range(RING)]
        hi_done, compared = sem("hi_done"), sem("compared")
        raw_in = [sem(f"raw_in{j}", unit=16) for j in range(2)]
        saved = [sem(f"saved{j}", unit=16) for j in range(2)]
        lo_done = sem("lo_done")
        s_in, s_done, peak_ps, peak_done = sem("s_in", unit=16), sem("s_done"), sem("peak_ps"), sem("peak_done")
        with nc.sbuf_tensor("f_raw", [P, RING, CH], F32) as raw, nc.sbuf_tensor("f_junk", [P, 2, CH], F32) as junk, \
             nc.sbuf_tensor("f_peaks", [P, 2, len(chunks)], F32) as peaks, \
             nc.sbuf_tensor("f_peak", [P, 1], F32) as peak, nc.sbuf_tensor("f_any", [1, 1], F32) as top, \
             ExitStack() as inner, nc.Block() as block:
            table = BiasTable(nc, inner, *bias, c, psum[1:4])

            @block.sync
            def _(sp):
                for n, (m, k) in enumerate(chunks):
                    if n >= RING:
                        sp.wait_ge(compared.sem, n - RING + 1)
                    sp.dma_start(raw[:, n % RING, 0:wide[m]], w[m + "_w"][k * P:(k + 1) * P])\
                      .then_inc(loaded[n % RING].sem, 16)

            @block.gpsimd
            def _(pool):
                pool.dma_start(ident[:], c["c_ident"]).then_inc(s_in.sem, 16)
                for dst, src in ((gate_s, "w1_s"), (both_s, "w2_s"), (h1_s, "h1_s"), (h2_s, "h2_s")):
                    pool.dma_start(dst[:], w[src]).then_inc(s_in.sem, 16)
                s3 = w["w3_s"]
                pool.dma_start(out_s[:], bass.AP(s3.tensor, s3.offset, [[0, P], [1, D]])).then_inc(s_in.sem, 16)
                table.move(pool)

            @block.scalar
            def _(act):
                for n, (m, k) in enumerate(chunks):
                    act.wait_ge(loaded[n % RING].sem, 16 * (n // RING + 1))
                    act.activation(hi[m][:, k], raw[:, n % RING, 0:wide[m]], ACT.Copy).then_inc(hi_done.sem, 1)
                    if n == len(chunks) // 2:
                        table.copies(act)

            @block.vector
            def _(dve):
                for n, (m, k) in enumerate(chunks):
                    dve.wait_ge(hi_done.sem, n + 1)
                    if n:
                        dve.wait_ge(compared.sem, n)
                    pair = raw[:, n % RING, 0:wide[m]], hi[m][:, k].bitcast(F32)
                    for sign in range(2):
                        ins = dve.tensor_tensor_reduce(junk[:, sign, 0:wide[m]], pair[sign], pair[1 - sign], 1.0, 0.0,
                                                       ALU.subtract, ALU.max, peaks[:, sign, n:n + 1])
                    ins.then_inc(compared.sem, 1)
                dve.wait_ge(compared.sem, len(chunks))
                dve.tensor_reduce(peak[:], peaks[:].rearrange("p a n -> p (a n)"), AX_X, ALU.max).then_inc(peak_done.sem, 1)
                dve.wait_ge(peak_ps.sem, 1)
                dve.tensor_reduce(top[:], psum[0][0:1, 0:P], AX_X, ALU.max).then_inc(peak_done.sem, 1)
                dve.wait_ge(peak_done.sem, 2)
                dve.tensor_scalar(flag[:], top[:], 0.0, None, ALU.is_gt)
                dve.wait_ge(s_in.sem, 16 * 6)
                dve.tensor_scalar(gate_s[:], gate_s[:], 0.5, None, ALU.mult).then_inc(s_done.sem, 1)
                dve.wait_ge(s_done.sem, 1)
                dve.tensor_tensor(both_s[:], gate_s[:], both_s[:], ALU.mult).then_inc(s_done.sem, 1)
                dve.wait_ge(s_done.sem, 2)

            @block.tensor
            def _(pe):
                table.products(pe)
                pe.wait_ge(s_in.sem, 16 * 6)
                pe.wait_ge(peak_done.sem, 1)
                pe.transpose(psum[0][0:1, 0:P], peak[:], ident[:]).then_inc(peak_ps.sem, 1)

        with nc.sbuf_tensor("f_raw2", [P, 2, CH], F32) as raw, nc.sbuf_tensor("f_lo", [P, 2, CH], F32) as lo, \
             nc.Block() as block:
            @block.sync
            def _(sp):
                with sp.If(sp.value_load(flag[0:1, 0:1], min_val=0, max_val=1) == 1):
                    for n, (m, k) in enumerate(chunks):
                        if n >= 2:
                            sp.wait_ge(lo_done.sem, n - 1)
                        sp.dma_start(raw[:, n % 2, 0:wide[m]], w[m + "_w"][k * P:(k + 1) * P])\
                          .then_inc(raw_in[n % 2].sem, 16)

            @block.vector
            def _(dve):
                with dve.If(dve.value_load(flag[0:1, 0:1], min_val=0, max_val=1) == 1):
                    for n, (m, k) in enumerate(chunks):
                        dve.wait_ge(raw_in[n % 2].sem, 16 * (n // 2 + 1))
                        if n >= 2:
                            dve.wait_ge(saved[n % 2].sem, 16 * (n // 2))
                        dve.tensor_tensor(lo[:, n % 2, 0:wide[m]], raw[:, n % 2, 0:wide[m]], hi[m][:, k].bitcast(F32),
                                          ALU.subtract).then_inc(lo_done.sem, 1)

            @block.scalar
            def _(act):
                with act.If(act.value_load(flag[0:1, 0:1], min_val=0, max_val=1) == 1):
                    for n, (m, k) in enumerate(chunks):
                        act.wait_ge(lo_done.sem, n + 1)
                        act.dma_start(lo_d[m][k * P:(k + 1) * P], lo[:, n % 2, 0:wide[m]]).then_inc(saved[n % 2].sem, 16)
                    for j in range(2):
                        act.wait_ge(saved[j].sem, 16 * (len(chunks) // 2))

        xh, xl = sb("xh", [P, KD, T], F32R), sb("xl", [P, KD, T], F32R)
        x_in, attn = sb("x_in", [P, TT, D]), sb("attn", [P, TT, D])
        out_sb = sb("out_sb", [P, TT, D])
        tanh = sb("tanh", [P, 2, T])
        gated = sb("gated", [P, 2, T])
        full = sb("full", [P, 2, T])
        hh = [sb(f"hh{j}", [P, KH, T], F32R) for j in range(2)]
        hl = [sb(f"hl{j}", [P, KH, T], F32R) for j in range(2)]

        xt_in, x_in_s = sem("xt_in", 2, unit=16), sem("x_in_s", 2, unit=16)
        gu_ps, t_done, gate_done = sem("gu_ps", KH), sem("t_done", KH), sem("gate_done", KH)
        h_full, h_hi, h_lo = sem("h_full", 2 * KH), sem("h_hi", 3 * KH), sem("h_lo", 3 * KH)
        h_ps, o_ps = sem("h_ps", 2 * KH), sem("o_ps", 2)
        scaled, added, out_done = sem("scaled", 2), sem("added", 1), sem("out_done", 2)
        out_saved = sem("out_saved", 1, grant=1, unit=16)
        lo_in = [sem("lo_in0", 2 * KH + 1, unit=16), sem("lo_in1", 2 * KH, unit=16)]
        lo_used = sem("lo_used", 4 * KH + 1, grant=1)
        half_gated = sem("half_gated", KH)

        gates, ups, hidden, outs = psum[0:2], psum[2:4], psum[4:6], psum[6:8]
        low_w3 = low[:].rearrange("p s k n -> p (s k n)").rearrange("p (k n) -> p k n", k=KH)
        STREAM = [(m, o) for o in range(KH) for m in ("w1", "w2")] + [("h1", o) for o in range(KH)] + \
                 [("h2", o) for o in range(KH)] + [("w3", 0)]

        with nc.Block() as block:
            @block.sync
            def _(sp):
                any_low = sp.value_load(flag[0:1, 0:1], min_val=0, max_val=1)

                def load(b):
                    sp.dma_start(xh[:].bitcast(F32), xh_d[b]).then_inc(xt_in.sem, 16)
                    sp.dma_start(xl[:].bitcast(F32), xl_d[b]).then_inc(xt_in.sem, 16)

                def load_sums(b):
                    sp.dma_start(x_in[:], x_d[b].rearrange("(t p) d -> p t d", p=P)).then_inc(x_in_s.sem, 16)
                    sp.dma_start(attn[:], attn_d[b].rearrange("(t p) d -> p t d", p=P)).then_inc(x_in_s.sem, 16)

                def batch(b):
                    load_sums(b)
                    with sp.If(any_low == 1):
                        for n, (m, o) in enumerate(STREAM):
                            sp.wait_ge(lo_used.sem, lo_used.at(n if m == "w3" else max(n - 1, 0), b))
                            src = lo_d[m].rearrange("(k p) n -> p k n", p=P)
                            if m == "w3":
                                dst = low_w3.bitcast(F32)
                            else:
                                dst, src = low[:, n % 2, 0:deep[m]].bitcast(F32), src[:, :, o * P:(o + 1) * P]
                            sp.dma_start(dst, src).then_inc(lo_in[n % 2].sem, 16)

                def store(b):
                    sp.wait_ge(out_done.sem, out_done.at(2, b))
                    sp.dma_start(out_d[b].rearrange("(t p) d -> p t d", p=P), out_sb[:]).then_inc(out_saved.sem, 16)

                load(0)
                with sp.Fori(0, B - 1) as i:
                    batch(i)
                    sp.wait_ge(gu_ps.sem, gu_ps.at(KH, i))
                    load(i + 1)
                    store(i)
                batch(B - 1)
                store(B - 1)
                sp.wait_ge(out_saved.sem, out_saved.at(1, B - 1))

            @block.gpsimd
            def _(pool):
                with pool.Fori(0, B) as i:
                    for n in range(3 * KH):
                        layer, o = n // KH, n % KH
                        if n == 2 * KH:
                            pool.wait_ge(x_in_s.sem, x_in_s.at(2, i))
                            pool.tensor_tensor(x_in[:], x_in[:], attn[:], ALU.add).then_inc(added.sem, 1)
                        pool.wait_ge(h_hi.sem, h_hi.at(n + 1, i))
                        pool.tensor_tensor(hl[layer % 2][:, o], full[:, n % 2], hh[layer % 2][:, o].bitcast(F32),
                                           ALU.subtract).then_inc(h_lo.sem, 1)

            @block.scalar
            def _(act):
                with act.Fori(0, B) as i:
                    for o in range(KH):
                        act.wait_ge(gu_ps.sem, gu_ps.at(o + 1, i))
                        if o >= 2:
                            act.wait_ge(gate_done.sem, gate_done.at(o - 1, i))
                        act.activation(tanh[:, o % 2], gates[o % 2][:], ACT.Tanh, scale=gate_s[:, o:o + 1])\
                           .then_inc(t_done.sem, 1)
                    for n in range(KH, 3 * KH):
                        layer, o = n // KH, n % KH
                        act.wait_ge(h_ps.sem, h_ps.at(n - KH + 1, i))
                        act.wait_ge(h_lo.sem, h_lo.at(n - 1, i))
                        act.activation(full[:, n % 2], hidden[n % 2][:], ACT.Gelu,
                                       scale=(h1_s if layer == 1 else h2_s)[:, o:o + 1]).then_inc(h_full.sem, 1)

            @block.vector
            def _(dve):
                dve.sem_inc(lo_used.sem, 1)
                dve.sem_inc(out_saved.sem, 16)
                with dve.Fori(0, B) as i:
                    for n in range(3 * KH):
                        layer, o = n // KH, n % KH
                        if layer == 0:
                            dve.wait_ge(t_done.sem, t_done.at(o + 1, i))
                            dve.scalar_tensor_tensor(gated[:, o % 2], tanh[:, o % 2], 1.0, gates[o % 2][:],
                                                     ALU.add, ALU.mult).then_inc(half_gated.sem, 1)
                            dve.wait_ge(half_gated.sem, half_gated.at(o + 1, i))
                            if o >= 2:
                                dve.wait_ge(h_lo.sem, h_lo.at(o - 1, i))
                            dve.scalar_tensor_tensor(full[:, o % 2], ups[o % 2][:], both_s[:, o:o + 1], gated[:, o % 2],
                                                     ALU.mult, ALU.mult).then_inc(gate_done.sem, 1)
                            dve.wait_ge(gate_done.sem, gate_done.at(o + 1, i))
                        else:
                            dve.wait_ge(h_full.sem, h_full.at(n - KH + 1, i))
                        dve.tensor_copy(hh[layer % 2][:, o], full[:, n % 2]).then_inc(h_hi.sem, 1)
                    dve.wait_ge(out_saved.sem, out_saved.at(0, i))
                    for m in range(2):
                        dve.wait_ge(o_ps.sem, o_ps.at(m + 1, i))
                        dst = out_sb[:, 2 * m:2 * m + 2]
                        dve.tensor_tensor(dst, outs[m][:].rearrange("p (t d) -> p t d", t=2),
                                          out_s[:].unsqueeze(1).to_broadcast([P, 2, D]), ALU.mult).then_inc(scaled.sem, 1)
                        dve.wait_ge(added.sem, added.at(1, i))
                        dve.wait_ge(scaled.sem, scaled.at(m + 1, i))
                        dve.tensor_tensor(dst, x_in[:, 2 * m:2 * m + 2], dst, ALU.add).then_inc(out_done.sem, 1)

            @block.tensor
            def _(pe):
                any_low = pe.value_load(flag[0:1, 0:1], min_val=0, max_val=1)

                def products(outs_, pairs, first, last):
                    for k in range(len(pairs[0])):
                        for out, ps in zip(outs_, pairs):
                            ins = pe.matmul(out, *ps[k], start=first and k == 0, stop=last and k == len(ps) - 1,
                                            skip_group_check=True)
                    return ins

                with pe.Fori(0, B) as i:
                    pe.wait_ge(xt_in.sem, xt_in.at(2, i))
                    for o in range(KH):
                        cut = slice(o * P, (o + 1) * P)
                        if o >= 2:
                            pe.wait_ge(gate_done.sem, gate_done.at(o - 1, i))
                        two = [gates[o % 2][:], ups[o % 2][:]]
                        products(two, [[(hi[m][:, k, cut], xl[:, k]) for k in range(KD)] for m in ("w1", "w2")], True, False)
                        with pe.If(any_low == 1):
                            for s in range(2):
                                pe.wait_ge(lo_in[s].sem, lo_in[s].at(o + 1, i))
                            products(two, [[(low[:, s, k], xh[:, k]) for k in range(KD)] for s in range(2)],
                                     False, False).then_inc(lo_used.sem, 2)
                        products(two, [[(hi[m][:, k, cut], xh[:, k]) for k in range(KD)] for m in ("w1", "w2")],
                                 False, True).then_inc(gu_ps.sem, 1)
                    for n in range(2 * KH):
                        layer, o = n // KH, n % KH
                        m, cut = ("h1", "h2")[layer], slice(o * P, (o + 1) * P)
                        high, lo_ = hh[layer % 2], hl[layer % 2]
                        if n >= 2:
                            pe.wait_ge(h_full.sem, h_full.at(n - 1, i))
                        out = hidden[n % 2][:]
                        for part, src, done in ((0, high, h_hi), (1, lo_, h_lo)):
                            for k in range(KH):
                                if o == 0:
                                    pe.wait_ge(done.sem, done.at(layer * KH + k + 1, i))
                                ins = pe.matmul(out, hi[m][:, k, cut], src[:, k], start=(part == 0 and k == 0),
                                                stop=(part == 1 and k == KH - 1), skip_group_check=True)
                            if part == 0:
                                with pe.If(any_low == 1):
                                    u = 2 * KH + n
                                    pe.wait_ge(lo_in[u % 2].sem, lo_in[u % 2].at(u // 2 + 1, i))
                                    products([out], [[(low[:, u % 2, k], high[:, k]) for k in range(KH)]],
                                             False, False).then_inc(lo_used.sem, 1)
                        ins.then_inc(h_ps.sem, 1)
                    high, lo_ = hh[0], hl[0]
                    for t in range(TT):
                        cut = slice(t * P, (t + 1) * P)
                        out = outs[t // 2][:, (t % 2) * D:(t % 2 + 1) * D]
                        for part, src, done in ((0, high, h_hi), (1, lo_, h_lo)):
                            for k in range(KH):
                                if t == 0:
                                    pe.wait_ge(done.sem, done.at(2 * KH + k + 1, i))
                                ins = pe.matmul(out, src[:, k, cut], hi["w3"][:, k], start=(part == 0 and k == 0),
                                                stop=(part == 1 and k == KH - 1), skip_group_check=True)
                            if part == 0:
                                with pe.If(any_low == 1):
                                    pe.wait_ge(lo_in[0].sem, lo_in[0].at(2 * KH + 1, i))
                                    last = products([out], [[(high[:, k, cut], low_w3[:, k]) for k in range(KH)]],
                                                    False, False)
                                    if t == TT - 1:
                                        last.then_inc(lo_used.sem, 1)
                        if t % 2:
                            ins.then_inc(o_ps.sem, 1)
        clear(nc, tallies)


def skewed(eng, front, middle, back):
    def after(b, s):
        return lambda t: middle(b, s, t)

    front(0, 0)
    for t in range(TT):
        middle(0, 0, t)
    for s in range(2):
        front(s + 1, (s + 1) % 2)
        back(s, s, after(s + 1, (s + 1) % 2))
    with eng.Fori(1, B // 2 - 1) as i:
        for s in range(2):
            front(i * 2 + (s + 1), (s + 1) % 2)
            back(i * 2 + s, s, after(i * 2 + (s + 1), (s + 1) % 2))
    front(B - 1, 1)
    back(B - 2, 0, after(B - 1, 1))
    back(B - 1, 1, lambda t: None)


def select(nc, sel, xh_d, xl_d, xn_d, pt_d, controller, c):
    with ExitStack() as ctx:
        def sb(name, shape, dt=F32):
            return ctx.enter_context(nc.sbuf_tensor(f"s_{name}", shape, dt))

        tallies = []

        def sem(name, per=0, grant=0, unit=1):
            tallies.append(Tally(ctx.enter_context(nc.semaphore(f"s_{name}")), per, grant, unit))
            return tallies[-1]

        G = P // NE
        ident, tie, parity, group = sb("ident", [P, P]), sb("tie", [P, T]), sb("parity", [P, T]), sb("group", [P, G])
        w_raw, w_low = sb("w_raw", [P, KD, P]), sb("w_low", [P, KD, P], F32R)
        w_high = sb("w_high", [P, KD, P], F32R)
        xh, xl = sb("xh", [P, 2, KD, T], F32R), sb("xl", [P, 2, KD, T], F32R)
        xn = sb("xn", [P, 2, TT, D])
        th, tl = sb("th", [P, 2, TT, D], F32R), sb("tl", [P, 2, TT, D], F32R)
        logits, best = sb("logits", [P, T]), sb("best", [P, T // NE])
        perm, picks = sb("perm", [P, 2, T]), sb("picks", [P, 2, T])
        blocks = sb("blocks", [P, 2, TT, G, E], F32R)
        banks = [ctx.enter_context(nc.psum_tensor(f"s_ps{j}", [P, T], F32)) for j in range(8)]
        lg_bank, tr_bank, sel_banks = banks[0], banks[1], banks[2:6]

        consts_in, w_hi, w_ready = sem("consts_in", unit=16), sem("w_hi"), sem("w_ready")
        xt_in = [sem(f"xt_in{s}", 2, unit=16) for s in range(2)]
        xn_in = [sem(f"xn_in{s}", 1, unit=16) for s in range(2)]
        pt_saved = [sem(f"pt_saved{s}", 1, unit=16) for s in range(2)]
        th_ready, tl_ready = sem("th_ready", 1), sem("tl_ready", 1)
        lg_ps, lg_ready, best_ready = sem("lg_ps", 1), sem("lg_ready", 1), sem("best_ready", 1)
        perm_ready, pt_ready = sem("perm_ready", 1), sem("pt_ready", 1)
        tr_ps, blocks_ready = sem("tr_ps", 1), sem("blocks_ready", TT)
        sel_ps = sem("sel_ps", 2 * TT)
        sel_done = [sem("sel_done0", TT), sem("sel_done1", TT)]

        def wait(eng, tally, k, b):
            value = tally.at(k, b)
            if not isinstance(value, int) or value > 0:
                eng.wait_ge(tally.sem, value)

        def nothing(b, s, t):
            pass

        def slot_wait(eng, tally, k, b, s):
            if isinstance(b, int):
                if tally.at(k, b // 2) > 0:
                    eng.wait_ge(tally.sem, tally.at(k, b // 2))
            else:
                eng.wait_ge(tally.sem, b * (tally.per // 2) + (tally.at(k) - s * (tally.per // 2)))

        with nc.Block() as block:
            @block.sync
            def _(sp):
                def front(b, s):
                    wait(sp, lg_ps, -1, b)
                    sp.dma_start(xh[:, s].bitcast(F32), xh_d[b]).then_inc(xt_in[s].sem, 16)
                    sp.dma_start(xl[:, s].bitcast(F32), xl_d[b]).then_inc(xt_in[s].sem, 16)
                    wait(sp, tl_ready, -1, b)
                    sp.dma_start(xn[:, s], xn_d[b]).then_inc(xn_in[s].sem, 16)

                skewed(sp, front, nothing, nothing)

            @block.gpsimd
            def _(pool):
                def front(b, s):
                    slot_wait(pool, xn_in[s], 1, b, s)
                    wait(pool, th_ready, 1, b)
                    wait(pool, sel_ps, 2 * TT, b - 2)
                    pool.tensor_tensor(tl[:, s], xn[:, s], th[:, s].bitcast(F32), ALU.subtract).then_inc(tl_ready.sem, 1)

                def back(b, s, after):
                    wait(pool, perm_ready, 1, b)
                    if not isinstance(b, int) or b >= 2:
                        slot_wait(pool, pt_saved[s], 0, b, s)
                    pool.tensor_tensor(picks[:, s], perm[:, s], parity[:], ALU.mult).then_inc(pt_ready.sem, 1)
                    wait(pool, pt_ready, 1, b)
                    pool.dma_start(pt_d[b], picks[:, s]).then_inc(pt_saved[s].sem, 16)
                pool.wait_ge(consts_in.sem, 16 * 6)
                skewed(pool, front, nothing, back)
                for s in range(2):
                    pool.wait_ge(pt_saved[s].sem, pt_saved[s].at(1, B // 2 - 1))

            @block.scalar
            def _(act):
                for twice in range(2):
                    act.dma_start(w_raw[:, :, twice * E:(twice + 1) * E],
                                  controller.rearrange("(k p) n -> p k n", p=P)).then_inc(consts_in.sem, 16)
                for dst, src in ((ident, "c_ident"), (tie, "c_tie"), (parity, "c_parity"), (group, "c_group")):
                    act.dma_start(dst[:], c[src]).then_inc(consts_in.sem, 16)

                def front(b, s):
                    slot_wait(act, xn_in[s], 1, b, s)
                    wait(act, sel_ps, 2 * TT, b - 2)
                    act.activation(th[:, s], xn[:, s], ACT.Copy).then_inc(th_ready.sem, 1)

                def back(b, s, after):
                    for t in range(TT):
                        n = 2 * t + 1
                        wait(act, sel_ps, n + 1, b)
                        act.activation(sel[:, 1, :, bass.ds(b * (TT * G) + t * G, G)],
                                       sel_banks[n % 4][:].rearrange("p (g e) -> p e g", g=G), ACT.Copy)\
                           .then_inc(sel_done[1].sem, 1)
                skewed(act, front, nothing, back)

            @block.vector
            def _(dve):
                dve.wait_ge(consts_in.sem, 16 * 6)
                dve.tensor_copy(w_high[:], w_raw[:]).then_inc(w_hi.sem, 1)
                dve.wait_ge(w_hi.sem, 1)
                dve.tensor_tensor(w_low[:], w_raw[:], w_high[:].bitcast(F32), ALU.subtract).then_inc(w_ready.sem, 1)

                def front(b, s):
                    wait(dve, best_ready, 0, b)
                    wait(dve, perm_ready, 0, b)
                    wait(dve, lg_ps, 1, b)
                    dve.tensor_tensor(logits[:], lg_bank[:], tie[:], ALU.add).then_inc(lg_ready.sem, 1)
                    wait(dve, lg_ready, 1, b)
                    grouped = logits[:].rearrange("p (g j) -> p g j", j=NE)
                    dve.tensor_reduce(best[:], grouped, AX_X, ALU.max).then_inc(best_ready.sem, 1)
                    wait(dve, best_ready, 1, b)
                    wait(dve, tr_ps, 1, b - 2)
                    wait(dve, pt_ready, 1, b - 2)
                    dve.tensor_tensor(perm[:, s].rearrange("p (g j) -> p g j", j=NE), grouped,
                                      best[:].unsqueeze(2).to_broadcast([P, T // NE, NE]), ALU.is_equal)\
                       .then_inc(perm_ready.sem, 1)

                def middle(b, s, t):
                    wait(dve, tr_ps, 1, b)
                    wait(dve, sel_ps, 2 * TT, b - 2)
                    dve.tensor_tensor(blocks[:, s, t], tr_bank[:, t * P:t * P + E].unsqueeze(1).to_broadcast([P, G, E]),
                                      group[:].unsqueeze(2).to_broadcast([P, G, E]), ALU.mult)\
                       .then_inc(blocks_ready.sem, 1)

                def back(b, s, after):
                    for t in range(TT):
                        wait(dve, sel_ps, 2 * t + 1, b)
                        dve.tensor_copy(sel[:, 0, :, bass.ds(b * (TT * G) + t * G, G)],
                                        sel_banks[2 * t % 4][:].rearrange("p (g e) -> p e g", g=G))\
                           .then_inc(sel_done[0].sem, 1)
                        if t >= TT // 2:
                            after(2 * t - TT)
                            after(2 * t - TT + 1)
                skewed(dve, front, middle, back)

            @block.tensor
            def _(pe):
                pe.wait_ge(w_ready.sem, 1)

                def front(b, s):
                    slot_wait(pe, xt_in[s], 2, b, s)
                    wait(pe, lg_ready, 0, b)
                    pairs = [(w, x[:, s, k]) for k in range(KD) for w, x in
                             ((w_high[:, k], xl), (w_low[:, k], xh), (w_high[:, k], xh))]
                    for m, (left, right) in enumerate(pairs):
                        ins = pe.matmul(lg_bank[:], left, right, start=m == 0, stop=m == len(pairs) - 1)
                    ins.then_inc(lg_ps.sem, 1)

                def middle(b, s, t):
                    if t == 0:
                        wait(pe, perm_ready, 1, b)
                        wait(pe, blocks_ready, 0, b)
                    ins = pe.transpose(tr_bank[:, t * P:(t + 1) * P], perm[:, s, t * P:(t + 1) * P], ident[:])
                    if t == TT - 1:
                        ins.then_inc(tr_ps.sem, 1)

                def back(b, s, after):
                    wait(pe, tl_ready, 1, b)
                    for n in range(2 * TT):
                        t, half = n // 2, n % 2
                        wait(pe, sel_done[half], t - 1, b)
                        wait(pe, blocks_ready, t + 1, b)
                        cut = slice(half * P, (half + 1) * P)
                        rhs = blocks[:, s, t].rearrange("p g e -> p (g e)")
                        out = sel_banks[n % 4][:]
                        pe.matmul(out, tl[:, s, t, cut], rhs, start=True, stop=False)
                        pe.matmul(out, th[:, s, t, cut], rhs, start=False, stop=True).then_inc(sel_ps.sem, 1)
                        if n == 3:
                            for u in range(TT):
                                after(u)
                skewed(pe, front, middle, back)


def experts(nc, sel, inter_d, f1, f2, bias, c):
    with ExitStack() as ctx:
        def sb(name, shape, dt=F32):
            return ctx.enter_context(nc.sbuf_tensor(f"e_{name}", shape, dt))

        tallies = []

        def sem(name, per=0, grant=0, unit=1):
            tallies.append(Tally(ctx.enter_context(nc.semaphore(f"e_{name}")), per, grant, unit))
            return tallies[-1]

        def slots(name, per):
            return [sem(f"{name}{s}", per, unit=16) for s in range(2)]

        R, GH, TURNS = 2, GROUPS // P, E // 4
        w1, w2 = sb("w1", [P, 2, KD, R * P]), sb("w2", [P, 2, R, 2, D])
        bias_sb = sb("bias", [ESZ, E])
        inner = sb("inner", [P, 2, GROUPS])
        stage = sb("stage", [P, 2, GH, R, 2 * D])
        banks = [ctx.enter_context(nc.psum_tensor(f"e_ps{j}", [P, T], F32)) for j in range(8)]
        in_banks, out_banks = banks[0:2], banks[4:8]

        bias_in, zeroed = sem("bias_in", unit=16), sem("zeroed")
        w1_in, w2_in, saved = slots("w1_in", 1), slots("w2_in", 2), slots("saved", GH)
        in_ps, inner_ready = sem("in_ps", R), sem("inner_ready", 2 * R)
        out_ps = sem("out_ps", GH * R)
        staged = [sem("staged0", R), sem("staged1", R)]

        def at(tally, k, i, s, back=0):
            return i * (2 * tally.per) + ((s - back) * tally.per + k * tally.unit)

        def wait(eng, tally, value):
            if not isinstance(value, int) or value > 0:
                eng.wait_ge(tally.sem, value)

        def loop(eng, body):
            for s in range(2):
                body(0, s)
            with eng.Fori(1, TURNS // 2) as i:
                for s in range(2):
                    body(i, s)

        def late(eng, hidden, output):
            def body(i, s):
                for j in range(R):
                    hidden(i, s, j)
                    if j:
                        output(i, s, j - 1)
                    elif s:
                        output(i, 0, R - 1)
                    elif not isinstance(i, int) or i:
                        output(i - 1, 1, R - 1)
            loop(eng, body)
            output(TURNS // 2 - 1, 1, R - 1)

        with nc.Block() as block:
            @block.sync
            def _(sp):
                sp.dma_start(bias_sb[:], bias).then_inc(bias_in.sem, 16)
                sp.wait_ge(zeroed.sem, 1)

                def body(i, s):
                    m = i * 2 + s
                    wait(sp, in_ps, at(in_ps, R, i, s, 2))
                    sp.dma_start(w1[:, s], f1[:, bass.ds(m * (R * P), R * P)].rearrange("(k p) n -> p k n", p=P))\
                      .then_inc(w1_in[s].sem, 16)
                    wait(sp, out_ps, at(out_ps, GH * R, i, s, 2))
                    src = f2[bass.ds(m * (R * P), R * P)].rearrange("(j a f) d -> a f j d", a=2, f=ESZ)
                    for a in range(2):
                        sp.dma_start(w2[a * ESZ:(a + 1) * ESZ, s, :, a], src[a]).then_inc(w2_in[s].sem, 16)
                loop(sp, body)

            @block.gpsimd
            def _(pool):
                def body(i, s):
                    m = i * 2 + s
                    for gh in range(GH):
                        wait(pool, staged[gh], at(staged[gh], R, i, s))
                        pool.dma_start(inter_d[gh * P:(gh + 1) * P, bass.ds(m * (2 * R), 2 * R)],
                                       stage[:, s, gh].rearrange("p j (a d) -> p (j a) d", a=2)).then_inc(saved[s].sem, 16)
                loop(pool, body)
                for s in range(2):
                    pool.wait_ge(saved[s].sem, saved[s].at(GH, TURNS // 2 - 1))

            @block.scalar
            def _(act):
                act.wait_ge(bias_in.sem, 16)

                def hidden(i, s, j):
                    wait(act, in_ps, at(in_ps, j + 1, i, s))
                    wait(act, out_ps, at(out_ps, GH * (j - 1), i, s))
                    for a in range(2):
                        act.activation(inner[a * ESZ:(a + 1) * ESZ, j % 2],
                                       in_banks[j % 2][0:ESZ, a * GROUPS:(a + 1) * GROUPS], ACT.Relu,
                                       bias=bias_sb[:, bass.ds((i * 2 + s) * (2 * R) + (2 * j + a), 1)])\
                           .then_inc(inner_ready.sem, 1)

                def output(i, s, j):
                    if j == 0:
                        wait(act, saved[s], saved[s].at(0, i))
                    wait(act, out_ps, at(out_ps, GH * j + 1, i, s))
                    act.activation(stage[:, s, 0, j], out_banks[j % 2 * 2][:], ACT.Copy).then_inc(staged[0].sem, 1)
                late(act, hidden, output)

            @block.vector
            def _(dve):
                dve.memset(w2[:], 0.0).then_inc(zeroed.sem, 1)

                def body(i, s):
                    for j in range(R):
                        if j == 0:
                            wait(dve, saved[s], saved[s].at(0, i))
                        wait(dve, out_ps, at(out_ps, GH * j + 2, i, s))
                        dve.tensor_copy(stage[:, s, 1, j], out_banks[j % 2 * 2 + 1][:]).then_inc(staged[1].sem, 1)
                loop(dve, body)

            @block.tensor
            def _(pe):
                def hidden(i, s, j):
                    if j == 0:
                        wait(pe, w1_in[s], w1_in[s].at(1, i))
                    wait(pe, inner_ready, at(inner_ready, 2 * (j - 1), i, s))
                    for a in range(2):
                        for k in range(KD):
                            rhs = sel[:, k, bass.ds((i * 2 + s) * (2 * R) + (2 * j + a), 1), :].rearrange("p a g -> p (a g)")
                            ins = pe.matmul(in_banks[j % 2][0:ESZ, a * GROUPS:(a + 1) * GROUPS],
                                            w1[:, s, k, j * P + a * ESZ:j * P + (a + 1) * ESZ], rhs,
                                            start=k == 0, stop=k == KD - 1, skip_group_check=True)
                    ins.then_inc(in_ps.sem, 1)

                def output(i, s, j):
                    if j == 0:
                        wait(pe, w2_in[s], w2_in[s].at(2, i))
                    wait(pe, inner_ready, at(inner_ready, 2 * (j + 1), i, s))
                    for gh in range(GH):
                        wait(pe, staged[gh], at(staged[gh], j - 1, i, s))
                        pe.matmul(out_banks[j % 2 * 2 + gh][:], inner[:, j % 2, gh * P:(gh + 1) * P],
                                  w2[:, s, j].rearrange("p a d -> p (a d)"), start=True, stop=True)\
                          .then_inc(out_ps.sem, 1)
                late(pe, hidden, output)


def combine(nc, inter_d, pt_d, x_d, attn_d, out_d):
    with ExitStack() as ctx:
        def sb(name, shape, dt=F32):
            return ctx.enter_context(nc.sbuf_tensor(f"c_{name}", shape, dt))

        tallies = []

        def sem(name, per=0, grant=0, unit=1):
            tallies.append(Tally(ctx.enter_context(nc.semaphore(f"c_{name}")), per, grant, unit))
            return tallies[-1]

        C = 4
        rows = sb("rows", [P, 2, TT, C, D])
        picks, x_in, attn = sb("picks", [P, 2, T]), sb("x_in", [P, 2, TT, D]), sb("attn", [P, 2, TT, D])
        out_sb = sb("out_sb", [P, 2, TT, D])
        banks = [ctx.enter_context(nc.psum_tensor(f"c_ps{j}", [P, T], F32)) for j in range(TT)]
        rows_in = [[sem(f"rows_in{s}{t}", 1, unit=16) for t in range(TT)] for s in range(2)]
        picks_in = [sem(f"picks_in{s}", 1, unit=16) for s in range(2)]
        sums_in = [sem(f"sums_in{s}", 2, unit=16) for s in range(2)]
        added, moe_ps, summed = sem("added", 1), sem("moe_ps", TT), sem("summed", TT)
        saved = [sem(f"saved{s}", 1, unit=16) for s in range(2)]

        def at(tally, k, i, s, back=0):
            return i * (2 * tally.per) + ((s - back) * tally.per + k * tally.unit)

        def wait(eng, tally, value):
            if not isinstance(value, int) or value > 0:
                eng.wait_ge(tally.sem, value)

        def loop(eng, body):
            for s in range(2):
                body(0, s)
            with eng.Fori(1, B // 2) as i:
                for s in range(2):
                    body(i, s)

        with nc.Block() as block:
            @block.sync
            def _(sp):
                def body(i, s):
                    b = i * 2 + s
                    wait(sp, moe_ps, at(moe_ps, TT, i, s, 2))
                    sp.dma_start(picks[:, s], pt_d[b]).then_inc(picks_in[s].sem, 16)
                    wait(sp, summed, at(summed, TT, i, s, 2))
                    for dst, src in ((x_in, x_d), (attn, attn_d)):
                        sp.dma_start(dst[:, s], src[b].rearrange("(t p) d -> p t d", p=P)).then_inc(sums_in[s].sem, 16)
                    src = inter_d[bass.ds(b * (T // NE), T // NE)].rearrange("(t c g) e d -> t (g e) c d", t=TT, c=C)
                    for t in range(TT):
                        sp.dma_start(rows[:, s, t], src[t]).then_inc(rows_in[s][t].sem, 16)
                loop(sp, body)

            @block.gpsimd
            def _(pool):
                def body(i, s):
                    wait(pool, sums_in[s], sums_in[s].at(2, i))
                    pool.tensor_tensor(x_in[:, s], x_in[:, s], attn[:, s], ALU.add).then_inc(added.sem, 1)
                loop(pool, body)

            @block.scalar
            def _(act):
                def body(i, s):
                    wait(act, summed, at(summed, TT, i, s))
                    act.dma_start(out_d[i * 2 + s].rearrange("(t p) d -> p t d", p=P), out_sb[:, s])\
                       .then_inc(saved[s].sem, 16)
                loop(act, body)
                for s in range(2):
                    act.wait_ge(saved[s].sem, saved[s].at(1, B // 2 - 1))

            @block.vector
            def _(dve):
                def body(i, s):
                    wait(dve, saved[s], saved[s].at(0, i))
                    wait(dve, added, at(added, 1, i, s))
                    for t in range(TT):
                        wait(dve, moe_ps, at(moe_ps, t + 1, i, s))
                        dve.tensor_tensor(out_sb[:, s, t], banks[t][:, 0:D], x_in[:, s, t], ALU.add).then_inc(summed.sem, 1)
                loop(dve, body)

            @block.tensor
            def _(pe):
                def body(i, s):
                    wait(pe, picks_in[s], picks_in[s].at(1, i))
                    for t in range(TT):
                        wait(pe, rows_in[s][t], rows_in[s][t].at(1, i))
                        wait(pe, summed, at(summed, t + 1, i, s, 1))
                        for g in range(C):
                            at32 = t * P + 32 * g
                            ins = pe.matmul(banks[t][32 * g:32 * g + 32, 0:D], picks[:, s, at32:at32 + 32], rows[:, s, t, g],
                                            start=True, stop=True, skip_group_check=True)
                        ins.then_inc(moe_ps.sem, 1)
                loop(pe, body)


_INS = ["L0_attn_x", "L0_attn_W_DKV", "L0_attn_W_UK", "L0_attn_W_UV", "L0_attn_W_UQ", "L0_attn_W_O",
        "L0_ffn_w1_w", "L0_ffn_w1_s", "L0_ffn_w2_w", "L0_ffn_w2_s", "L0_ffn_h1_w", "L0_ffn_h1_s",
        "L0_ffn_h2_w", "L0_ffn_h2_s", "L0_ffn_w3_w", "L0_ffn_w3_s", "L1_attn_Wqkv", "L1_attn_Wout",
        "L1_attn_Wpos", "L1_attn_coeffs", "L1_ffn_controller", "L1_ffn_f1", "L1_ffn_f2", "L1_ffn_bias"]
_TRANSPOSED = {"L0_ffn_w1_w", "L0_ffn_w2_w", "L0_ffn_h1_w", "L0_ffn_h2_w", "L0_ffn_w3_w", "L1_attn_Wqkv",
               "L1_attn_Wout", "L1_attn_Wpos", "L1_ffn_bias"}
_FLAT = {"L1_ffn_controller": (D, E), "L1_ffn_f1": (D, E * ESZ), "L1_ffn_f2": (E * ESZ, D), "L1_ffn_bias": (E, ESZ)}
_BY_TILE = {"L0_ffn_w1_s", "L0_ffn_w2_s", "L0_ffn_h1_s", "L0_ffn_h2_s"}


def program(nc, a, out, c):
    def scratch(name, shape, dt=F32):
        return nc.dram_tensor(name, shape, dt, kind=SCRATCH).ap()

    xh_d, xl_d = scratch("xh", [B, P, KD, T]), scratch("xl", [B, P, KD, T])
    attn_d = scratch("attn", [B, T, D])

    def place0(name, stage, ap):
        if name in "kv":
            return [(stage[r:r + LATENT, 0], ap) for r in (0, LATENT)]
        return [(stage[:, :, 0:ap.shape[1]], ap.rearrange("(k p) n -> p k n", p=P))]

    w0 = {"loads": [("q", a["L0_attn_W_UQ"]), ("k", a["L0_attn_W_UK"]), ("v", a["L0_attn_W_UV"]),
                    ("c", a["L0_attn_W_DKV"])], "wo": a["L0_attn_W_O"], "place": place0}
    attention(nc, "l0", 0, a["L0_attn_x"], attn_d, xh_d, xl_d, None, w0, c)
    x1_d, ext_d = scratch("x1", [B, T, D]), scratch("ext", [H, 2 * T])
    lo_d = {m: scratch(f"lo_{m}", list(a[f"L0_ffn_{m}_w"].shape)) for m in ("w1", "w2", "h1", "h2", "w3")}
    ffn(nc, a["L0_attn_x"], attn_d, xh_d, xl_d, x1_d, {k[7:]: v for k, v in a.items() if k.startswith("L0_ffn_")}, c, lo_d,
        (a["L1_attn_Wpos"], a["L1_attn_coeffs"], ext_d))

    def place1(name, stage, ap):
        return [(stage[:, :, 0:D], ap.rearrange("(k p) n -> p k n", p=P))]

    yh_d, yl_d, yn_d = scratch("yh", [B, P, KD, T]), scratch("yl", [B, P, KD, T]), scratch("yn", [B, P, TT, D])
    attn1_d = scratch("attn1", [B, T, D])
    wqkv = a["L1_attn_Wqkv"]
    w1 = {"loads": [(name, wqkv[:, n * D:(n + 1) * D]) for n, name in enumerate("qkv")],
          "wo": a["L1_attn_Wout"], "place": place1, "ext": ext_d}
    attention(nc, "l1", 1, x1_d, attn1_d, yh_d, yl_d, yn_d, w1, c)
    pt_d, inter_d = scratch("pt", [B, P, T]), scratch("inter", [GROUPS, E, D])
    with nc.sbuf_tensor("sel", [P, KD, E, GROUPS], F32) as sel:
        select(nc, sel, yh_d, yl_d, yn_d, pt_d, a["L1_ffn_controller"], c)
        experts(nc, sel, inter_d, a["L1_ffn_f1"], a["L1_ffn_f2"], a["L1_ffn_bias"], c)
    combine(nc, inter_d, pt_d, x1_d, attn1_d, out)


SCRATCH = "Internal"


def kernel(**inputs):
    import concourse.bacc as _bacc
    from concourse.bass_utils import run_bass_kernel_spmd as _run

    nc = _bacc.Bacc("TRN2", target_bir_lowering=False, num_devices=1)
    arrays, aps, cs = {}, {}, {}
    for name in _INS:
        x = np.asarray(inputs[name])
        if name in _FLAT:
            x = x.reshape(_FLAT[name])
        if name in _BY_TILE:
            x = x.reshape(-1, P).T
        arrays[f"in_{name}"] = np.ascontiguousarray(x.T if name in _TRANSPOSED else x)
    arrays.update(consts())
    for name, x in arrays.items():
        ap = nc.dram_tensor(name, x.shape, mybir.dt.from_np(x.dtype), kind="ExternalInput").ap()
        (cs if name.startswith("c_") else aps)[name.removeprefix("in_")] = ap
    out = nc.dram_tensor("out", (B, T, D), F32, kind="ExternalOutput").ap()
    program(nc, aps, out, cs)
    r = _run(nc, [arrays], core_ids=[0])
    return r.results[0]["out"]
```
